# Optimizing a Trainium2 kernel written in Bass

```python
import numpy as np
import jax
import jax.numpy as jnp

def _softmax(x, axis=-1):
    return jax.nn.softmax(x, axis=axis)

def _gelu(x):
    return jax.nn.gelu(x, approximate=True)

def _silu(x):
    return jax.nn.silu(x)

def _sigmoid(x):
    return jax.nn.sigmoid(x)

def _layernorm(x, axis=-1, eps=1e-05):
    m = jnp.mean(x, axis=axis, keepdims=True)
    v = jnp.var(x, axis=axis, keepdims=True)
    return (x - m) / jnp.sqrt(v + eps)

def _scatter_add(tgt, idx, src, axis=0):
    return tgt.at[idx].add(src)

def _segment_sum(src, seg, n):
    return jax.ops.segment_sum(src, seg, n)
kernel_name = 'mk_decoder_postln_d1_seqx_r4_05650b'

def setup_inputs(seed: int=0):
    np.random.seed(seed)
    _w = jnp.asarray

    def _rec_inputs():
        import jax
        import jax.numpy as jnp
        _rk = jax.random.key(seed)
        x = -0.0003929 + 0.9999 * jax.random.normal(jax.random.fold_in(_rk, 1), (4, 512, 512), jnp.float32)
        _lenS = 512 - jax.random.randint(jax.random.fold_in(_rk, 7), (4,), 0, max(1, 512 // 4) + 1, jnp.int32)
        _lenS2 = 1601 - jax.random.randint(jax.random.fold_in(_rk, 8), (4,), 0, max(1, 1601 // 4) + 1, jnp.int32)
        _ctx_2048P = jax.random.normal(jax.random.fold_in(_rk, 11), (4, 16, 512), jnp.float32)
        _ctx_2048c = jax.random.dirichlet(jax.random.fold_in(_rk, 511), 0.3 * jnp.ones((16,), jnp.float32), (4, 1601))
        _ctx_2048t = jnp.einsum('bsk,bkd->bsd', _ctx_2048c, _ctx_2048P)
        _ctx_2048t = _ctx_2048t * jax.lax.rsqrt(jnp.mean(jnp.square(_ctx_2048t)) + 1e-12) * 0.953939
        ctx_2048 = -0.000514642 + 1.00011 * (_ctx_2048t + 0.3 * jax.random.normal(jax.random.fold_in(_rk, 611), (4, 1601, 512), jnp.float32))
        return (x, ctx_2048)
    x, ctx_2048 = _rec_inputs()

    def _L0_attn_setup():
        import jax, jax.numpy as jnp
        import numpy as np
        EPS = 1e-05
        key = jax.random.key(seed)
        ks = jax.random.split(key, 6)
        B, T, H = (4, 512, 512)
        scale = 2 ** (-2.5) * (6.0 / (H + H)) ** 0.5
        return {'hidden_states': jax.random.normal(ks[0], (B, T, H), dtype=jnp.float32), 'Wi': jax.random.normal(ks[1], (H, H), dtype=jnp.float32) * scale, 'Wf': jax.random.normal(ks[2], (H, H), dtype=jnp.float32) * scale, 'Wg': jax.random.normal(ks[3], (H, H), dtype=jnp.float32) * scale, 'Wo': jax.random.normal(ks[4], (H, H), dtype=jnp.float32) * scale, 'gnorm_w': jnp.ones((H,), dtype=jnp.float32)}
    _L0_attn_all = _L0_attn_setup()
    _L0_attn_in = {k: v for k, v in _L0_attn_all.items() if k in ('Wi', 'Wf', 'Wg', 'Wo', 'gnorm_w')}
    del _L0_attn_all

    def _L0_xattn_setup():
        import jax, jax.numpy as jnp
        import numpy as np
        DIM = 512
        NHEADS = 32
        HEAD_DIM = DIM // NHEADS
        EPS = 1e-06

        def _rmsnorm(t):
            return t * jax.lax.rsqrt(jnp.mean(t * t, axis=-1, keepdims=True) + EPS)
        key = jax.random.key(seed)
        kx, kc, kq, kk, kv = jax.random.split(key, 5)
        x = jax.random.normal(kx, (2, 1024, DIM), dtype=jnp.float32)
        context = jax.random.normal(kc, (2, 128, DIM), dtype=jnp.float32)
        std = 0.02
        Wq = jax.random.normal(kq, (DIM, DIM), dtype=jnp.float32) * std
        Wk = jax.random.normal(kk, (DIM, DIM), dtype=jnp.float32) * std
        Wv = jax.random.normal(kv, (DIM, DIM), dtype=jnp.float32) * std
        return {'x': x, 'context': context, 'Wq': Wq, 'Wk': Wk, 'Wv': Wv}
    _L0_xattn_all = _L0_xattn_setup()
    _L0_xattn_in = {k: v for k, v in _L0_xattn_all.items() if k in ('Wq', 'Wk', 'Wv')}
    del _L0_xattn_all

    def _L0_ffn_setup():
        import jax, jax.numpy as jnp
        import numpy as np
        HID = 512
        N_HEADS = 16
        N_KV = 16
        HEAD_DIM = HID // N_HEADS
        N_EXP = 8
        TOP_K = 2
        MOE_I = 352
        SH_I = 1408
        EPS = 1e-06
        ROPE_THETA = 1000000.0

        def _rms(x, w):
            v = jnp.mean(jnp.square(x), axis=-1, keepdims=True)
            return x * jax.lax.rsqrt(v + EPS) * w

        def _rope(q, k):
            S, D = (q.shape[1], q.shape[-1])
            inv = 1.0 / ROPE_THETA ** (jnp.arange(0, D, 2, dtype=jnp.float32) / D)
            freqs = jnp.arange(S, dtype=jnp.float32)[:, None] * inv[None, :]
            emb = jnp.concatenate([freqs, freqs], axis=-1)
            cos = jnp.cos(emb)[None, :, None, :]
            sin = jnp.sin(emb)[None, :, None, :]

            def rot(t):
                t1, t2 = (t[..., :D // 2], t[..., D // 2:])
                return jnp.concatenate([-t2, t1], axis=-1)
            return (q * cos + rot(q) * sin, k * cos + rot(k) * sin)
        key = jax.random.key(seed)
        ks = jax.random.split(key, 20)
        s = 0.02
        d = {'x': jax.random.normal(ks[0], (2, 256, HID), jnp.float32), 'w_ln1': jnp.ones((HID,), jnp.float32), 'wq': jax.random.normal(ks[1], (HID, N_HEADS * HEAD_DIM), jnp.float32) * s, 'bq': jnp.zeros((N_HEADS * HEAD_DIM,), jnp.float32), 'wk': jax.random.normal(ks[2], (HID, N_KV * HEAD_DIM), jnp.float32) * s, 'bk': jnp.zeros((N_KV * HEAD_DIM,), jnp.float32), 'wv': jax.random.normal(ks[3], (HID, N_KV * HEAD_DIM), jnp.float32) * s, 'bv': jnp.zeros((N_KV * HEAD_DIM,), jnp.float32), 'wo': jax.random.normal(ks[4], (N_HEADS * HEAD_DIM, HID), jnp.float32) * s, 'w_ln2': jnp.ones((HID,), jnp.float32), 'w_router': jax.random.normal(ks[5], (HID, N_EXP), jnp.float32) * s, 'w_gate_e': jax.random.normal(ks[6], (N_EXP, HID, MOE_I), jnp.float32) * s, 'w_up_e': jax.random.normal(ks[7], (N_EXP, HID, MOE_I), jnp.float32) * s, 'w_down_e': jax.random.normal(ks[8], (N_EXP, MOE_I, HID), jnp.float32) * s, 'w_sh_gate': jax.random.normal(ks[9], (HID, SH_I), jnp.float32) * s, 'w_sh_up': jax.random.normal(ks[10], (HID, SH_I), jnp.float32) * s, 'w_sh_down': jax.random.normal(ks[11], (SH_I, HID), jnp.float32) * s, 'w_sh_eg': jax.random.normal(ks[12], (HID, 1), jnp.float32) * s}
        return d
    _L0_ffn_all = _L0_ffn_setup()
    _L0_ffn_in = {k: v for k, v in _L0_ffn_all.items() if k in ('w_ln1', 'wq', 'bq', 'wk', 'bk', 'wv', 'bv', 'wo', 'w_ln2', 'w_router', 'w_gate_e', 'w_up_e', 'w_down_e', 'w_sh_gate', 'w_sh_up', 'w_sh_down', 'w_sh_eg')}
    del _L0_ffn_all
    return {'x': x, 'ctx_2048': ctx_2048, 'L0_attn_Wi': _L0_attn_in['Wi'], 'L0_attn_Wf': _L0_attn_in['Wf'], 'L0_attn_Wg': _L0_attn_in['Wg'], 'L0_attn_Wo': _L0_attn_in['Wo'], 'L0_attn_gnorm_w': _L0_attn_in['gnorm_w'], 'L0_xattn_Wq': _L0_xattn_in['Wq'], 'L0_xattn_Wk': _L0_xattn_in['Wk'], 'L0_xattn_Wv': _L0_xattn_in['Wv'], 'L0_ffn_w_ln1': _L0_ffn_in['w_ln1'], 'L0_ffn_wq': _L0_ffn_in['wq'], 'L0_ffn_bq': _L0_ffn_in['bq'], 'L0_ffn_wk': _L0_ffn_in['wk'], 'L0_ffn_bk': _L0_ffn_in['bk'], 'L0_ffn_wv': _L0_ffn_in['wv'], 'L0_ffn_bv': _L0_ffn_in['bv'], 'L0_ffn_wo': _L0_ffn_in['wo'], 'L0_ffn_w_ln2': _L0_ffn_in['w_ln2'], 'L0_ffn_w_router': _L0_ffn_in['w_router'], 'L0_ffn_w_gate_e': _L0_ffn_in['w_gate_e'], 'L0_ffn_w_up_e': _L0_ffn_in['w_up_e'], 'L0_ffn_w_down_e': _L0_ffn_in['w_down_e'], 'L0_ffn_w_sh_gate': _L0_ffn_in['w_sh_gate'], 'L0_ffn_w_sh_up': _L0_ffn_in['w_sh_up'], 'L0_ffn_w_sh_down': _L0_ffn_in['w_sh_down'], 'L0_ffn_w_sh_eg': _L0_ffn_in['w_sh_eg']}

def reference(x, ctx_2048, L0_attn_Wi, L0_attn_Wf, L0_attn_Wg, L0_attn_Wo, L0_attn_gnorm_w, L0_xattn_Wq, L0_xattn_Wk, L0_xattn_Wv, L0_ffn_w_ln1, L0_ffn_wq, L0_ffn_bq, L0_ffn_wk, L0_ffn_bk, L0_ffn_wv, L0_ffn_bv, L0_ffn_wo, L0_ffn_w_ln2, L0_ffn_w_router, L0_ffn_w_gate_e, L0_ffn_w_up_e, L0_ffn_w_down_e, L0_ffn_w_sh_gate, L0_ffn_w_sh_up, L0_ffn_w_sh_down, L0_ffn_w_sh_eg):
    import jax
    import jax.numpy as jnp

    def _L0_attn_ref(hidden_states, Wi, Wf, Wg, Wo, gnorm_w):
        import jax, jax.numpy as jnp
        import numpy as np
        EPS = 1e-05
        i = jnp.einsum('bth,dh->btd', hidden_states, Wi)
        f = jnp.einsum('bth,dh->btd', hidden_states, Wf)
        g = jnp.einsum('bth,dh->btd', hidden_states, Wg)
        gate = jax.nn.sigmoid(f)
        v = jax.nn.silu(i) * (1.0 - gate)

        def combine(c1, c2):
            a1, b1 = c1
            a2, b2 = c2
            return (a1 * a2, a2 * b1 + b2)
        _, o = jax.lax.associative_scan(combine, (gate, v), axis=1)
        rms = o * jax.lax.rsqrt(jnp.mean(o * o, axis=-1, keepdims=True) + EPS)
        o = rms * gnorm_w * g * jax.nn.sigmoid(g)
        return jnp.einsum('btd,hd->bth', o, Wo)

    def _L0_xattn_ref(x, context, Wq, Wk, Wv):
        import jax, jax.numpy as jnp
        import numpy as np
        DIM = 512
        NHEADS = 32
        HEAD_DIM = DIM // NHEADS
        EPS = 1e-06

        def _rmsnorm(t):
            return t * jax.lax.rsqrt(jnp.mean(t * t, axis=-1, keepdims=True) + EPS)
        b, n, _ = x.shape
        m = context.shape[1]
        q = x @ Wq.T
        k_raw = context @ Wk.T
        v_raw = context @ Wv.T
        q = q.reshape(b, n, NHEADS, HEAD_DIM).transpose(0, 2, 1, 3)
        kv = jnp.concatenate([k_raw, v_raw], axis=-1)
        kv = kv.reshape(b, m, NHEADS, HEAD_DIM, 2)
        k = kv[..., 0].transpose(0, 2, 1, 3)
        v = kv[..., 1].transpose(0, 2, 1, 3)
        q = _rmsnorm(q)
        k = _rmsnorm(k)
        scale = HEAD_DIM ** (-0.5)
        scores = jnp.einsum('bhnd,bhmd->bhnm', q, k) * scale
        attn = jax.nn.softmax(scores, axis=-1)
        out = jnp.einsum('bhnm,bhmd->bhnd', attn, v)
        return out.transpose(0, 2, 1, 3).reshape(b, n, NHEADS * HEAD_DIM)

    def _L0_ffn_ref(x, w_ln1, wq, bq, wk, bk, wv, bv, wo, w_ln2, w_router, w_gate_e, w_up_e, w_down_e, w_sh_gate, w_sh_up, w_sh_down, w_sh_eg):
        import jax, jax.numpy as jnp
        import numpy as np
        HID = 512
        N_HEADS = 16
        N_KV = 16
        HEAD_DIM = HID // N_HEADS
        N_EXP = 8
        TOP_K = 2
        MOE_I = 352
        SH_I = 1408
        EPS = 1e-06
        ROPE_THETA = 1000000.0

        def _rms(x, w):
            v = jnp.mean(jnp.square(x), axis=-1, keepdims=True)
            return x * jax.lax.rsqrt(v + EPS) * w

        def _rope(q, k):
            S, D = (q.shape[1], q.shape[-1])
            inv = 1.0 / ROPE_THETA ** (jnp.arange(0, D, 2, dtype=jnp.float32) / D)
            freqs = jnp.arange(S, dtype=jnp.float32)[:, None] * inv[None, :]
            emb = jnp.concatenate([freqs, freqs], axis=-1)
            cos = jnp.cos(emb)[None, :, None, :]
            sin = jnp.sin(emb)[None, :, None, :]

            def rot(t):
                t1, t2 = (t[..., :D // 2], t[..., D // 2:])
                return jnp.concatenate([-t2, t1], axis=-1)
            return (q * cos + rot(q) * sin, k * cos + rot(k) * sin)
        B, S, H = x.shape
        h = _rms(x, w_ln1)
        q = (h @ wq + bq).reshape(B, S, N_HEADS, HEAD_DIM)
        k = (h @ wk + bk).reshape(B, S, N_KV, HEAD_DIM)
        v = (h @ wv + bv).reshape(B, S, N_KV, HEAD_DIM)
        q, k = _rope(q, k)
        rep = N_HEADS // N_KV
        if rep > 1:
            k = jnp.repeat(k, rep, axis=2)
            v = jnp.repeat(v, rep, axis=2)
        scores = jnp.einsum('bqhd,bkhd->bhqk', q, k) * HEAD_DIM ** (-0.5)
        causal = jnp.tril(jnp.ones((S, S), bool))
        scores = jnp.where(causal[None, None], scores, jnp.finfo(scores.dtype).min)
        attn = jax.nn.softmax(scores, axis=-1)
        ctx = jnp.einsum('bhqk,bkhd->bqhd', attn, v).reshape(B, S, N_HEADS * HEAD_DIM)
        x = x + ctx @ wo
        h = _rms(x, w_ln2).reshape(B * S, H)
        logits = h @ w_router
        probs = jax.nn.softmax(logits, axis=-1)
        top_w, top_i = jax.lax.top_k(probs, TOP_K)
        combine = jnp.sum(jax.nn.one_hot(top_i, N_EXP, dtype=h.dtype) * top_w[..., None], axis=1)
        g = jnp.einsum('th,ehi->eti', h, w_gate_e)
        u = jnp.einsum('th,ehi->eti', h, w_up_e)
        y = jnp.einsum('eti,eih->eth', jax.nn.silu(g) * u, w_down_e)
        routed = jnp.einsum('eth,te->th', y, combine)
        sh = jax.nn.silu(h @ w_sh_gate) * (h @ w_sh_up) @ w_sh_down
        sh = sh * jax.nn.sigmoid(h @ w_sh_eg)
        x = x + (routed + sh).reshape(B, S, H)
        return x
    x = _layernorm(x + _L0_attn_ref(x, L0_attn_Wi, L0_attn_Wf, L0_attn_Wg, L0_attn_Wo, L0_attn_gnorm_w), axis=-1)
    x = _layernorm(x + _L0_xattn_ref(x, ctx_2048, L0_xattn_Wq, L0_xattn_Wk, L0_xattn_Wv), axis=-1)
    x = _layernorm(x + _L0_ffn_ref(x, L0_ffn_w_ln1, L0_ffn_wq, L0_ffn_bq, L0_ffn_wk, L0_ffn_bk, L0_ffn_wv, L0_ffn_bv, L0_ffn_wo, L0_ffn_w_ln2, L0_ffn_w_router, L0_ffn_w_gate_e, L0_ffn_w_up_e, L0_ffn_w_down_e, L0_ffn_w_sh_gate, L0_ffn_w_sh_up, L0_ffn_w_sh_down, L0_ffn_w_sh_eg), axis=-1)
    return x

_drawn_inputs = setup_inputs


def setup_inputs(seed=0):
    import zlib

    import numpy as np

    out = dict(_drawn_inputs(seed))
    spreads = {'L0_attn_gnorm_w': (1.0, 0.6),
     'L0_ffn_w_ln1': (1.0, 0.6),
     'L0_ffn_bq': (0.0, 0.8),
     'L0_ffn_bk': (0.0, 0.8),
     'L0_ffn_bv': (0.0, 0.356),
     'L0_ffn_w_ln2': (1.0, 0.6)}
    factors = {'L0_attn_Wf': 7.241,
     'L0_ffn_wq': 8.0,
     'L0_ffn_wk': 8.0,
     'L0_ffn_w_router': 8.0,
     'L0_ffn_w_gate_e': 8.0,
     'L0_ffn_w_up_e': 8.0,
     'L0_ffn_w_down_e': 8.0,
     'L0_ffn_w_sh_eg': 64.0,
     'L0_ffn_w_sh_gate': 8.0,
     'L0_ffn_w_sh_up': 8.0,
     'L0_ffn_w_sh_down': 8.0}
    for name, (base, spread) in spreads.items():
        noise = np.random.default_rng([zlib.crc32(name.encode()), seed]).standard_normal(out[name].shape)
        drawn = base * np.exp(spread * noise) if base else spread * noise
        out[name] = jnp.asarray(drawn.astype(out[name].dtype))
    for name, factor in factors.items():
        out[name] = (out[name] * factor).astype(out[name].dtype)
    return out
```

```python
from contextlib import ExitStack

import numpy as np

import concourse.bass as bass
from concourse import mybir

F32 = mybir.dt.float32
F32R = mybir.dt.float32r
BF16 = mybir.dt.bfloat16
ALU = mybir.AluOpType
ACT = mybir.ActivationFunctionType
AX_X = mybir.AxisListType.X

P = 128
B, T, H = 4, 512, 512
KC = H // P
TT = T // P
N = 512

XH, XD = 32, 16
CTX = 1601
CT = -(-CTX // P)
LAST = CTX - (CT - 1) * P
HH = XH // 2
HG = 4
NG = HH // HG
SPLIT_ROWS = 6 * XD

SH, SD = 16, 32
NEXP, MI, SI = 8, 352, 1408
NE = NEXP + SI // MI
IT = [(0, 128), (128, 128), (256, 96)]


class Count:

    def __init__(self, eng, sem, base=0):
        self.eng, self.sem, self.base, self.n = eng, sem, base, 0

    def done(self, ins):
        ins.then_inc(self.sem, 1)
        self.n += 1
        return self.n

    def wait(self, n=None):
        self.eng.wait_ge(self.sem, self.base + (self.n if n is None else n))


def apart(eng, sem, value, s_apart):
    eng.wait_ge(sem, value)
    eng.sem_inc(s_apart, 1)


def one(ap):
    return ap.rearrange("p o n -> p (o n)")


class Memory:

    def __init__(self, nc, stack, tag=""):
        self.nc, self.stack, self.tag, self.sems = nc, stack, tag, []
        stack.callback(self.clear)

    def sb(self, name, shape, dt=F32):
        return self.stack.enter_context(self.nc.sbuf_tensor(self.tag + name, shape, dt))

    def banks(self):
        psum = self.stack.enter_context(self.nc.psum_tensor(self.tag + "psum", [P, 8, N], F32))
        return psum, [psum[:, i, :] for i in range(8)]

    def sem(self, *names):
        got = [self.nc.alloc_semaphore(self.tag + n) for n in names]
        self.sems += got
        return got if len(got) > 1 else got[0]

    def clear(self):
        if not self.sems:
            return
        self.nc.clear_and_free_semaphores(self.sems)
        self.nc.all_engine_barrier()


def identities(nc, ident, ident16):
    with ExitStack() as stack:
        s_id = Memory(nc, stack).sem("identity")
        block = stack.enter_context(nc.Block())

        @block.gpsimd
        def _(pool):
            for i, t in enumerate((ident, ident16)):
                pool.memset(t[:], 0.0).then_inc(s_id, 1)
                pool.wait_ge(s_id, 2 * i + 1)
                pool.affine_select(out=t[:], in_=t[:], compare_op=ALU.not_equal, fill=1.0, base=0,
                                   pattern=[[-1, P]], channel_multiplier=1).then_inc(s_id, 1)


def product3(pe, out, lhs_hi, lhs_lo, rhs_hi, rhs_lo, chunks, first=True, last=True):
    terms = [(a, b) for c in range(chunks) for a, b in ((lhs_hi, rhs_hi), (lhs_hi, rhs_lo), (lhs_lo, rhs_hi))]
    for i, (a, b) in enumerate(terms):
        c = i // 3
        mm = pe.matmul(out, a(c), b(c), start=first and i == 0, stop=last and i == len(terms) - 1)
    return mm


def layernorm(dve, X, row, stats, mv, ve, rstd, own, s_ve, s_rstd, s_apart, it, tiles=TT):
    for t in range(tiles):
        own.done(dve.bn_stats(stats[:, t, :], one(X[:, bass.ds(row(t), 1), :])))
    apart(dve, own.sem, own.base + own.n, s_apart)
    for t in range(tiles):
        own.done(dve.bn_aggr(mv[:, t, :], stats[:, t, :]))
    own.wait()
    dve.tensor_scalar(ve[:], mv[:, :, 1], 1e-5, None, ALU.add).then_inc(s_ve, 1)
    dve.wait_ge(s_rstd, it + 1)
    for t in range(tiles):
        xt = one(X[:, bass.ds(row(t), 1), :])
        own.done(dve.tensor_scalar(xt, xt, mv[:, t, 0:1], rstd[:, t:t + 1], ALU.subtract, ALU.mult))
    own.wait()


def hgrn(nc, X, ident, d):
    with ExitStack() as stack:
        m = Memory(nc, stack, "r_")
        w_raw = [m.sb(f"w_raw{i}", [P, KC, H]) for i in range(2)]
        w_hi = [m.sb(f"w_hi{i}", [P, KC, H], F32R) for i in range(4)]
        w_lo = [m.sb(f"w_lo{i}", [P, KC, H], F32R) for i in range(4)]
        gw = m.sb("gw", [P, KC])
        x_raw = m.sb("x_raw", [P, KC, T])
        x_hi = m.sb("x_hi", [P, KC, T], F32R)
        x_lo = m.sb("x_lo", [P, KC, T], F32R)
        o_hi = m.sb("o_hi", [P, KC, T], F32R)
        o_lo = m.sb("o_lo", [P, KC, T], F32R)
        sig = m.sb("sig", [P, 2, 4, T])
        v = m.sb("v", [P, T])
        o = m.sb("o", [P, 2, T])
        sg = m.sb("sg", [P, T])
        og = m.sb("og", [P, 2, T])
        osq = m.sb("osq", [P, T])
        sumsq = m.sb("sumsq", [P, 2, T])
        ones = m.sb("ones", [P, 1])
        half = m.sb("half", [P, TT])
        ms = m.sb("ms", [P, TT])
        rr = m.sb("rr", [P, TT])
        stats = m.sb("stats", [P, TT, 6])
        mv = m.sb("mv", [P, TT, 2])
        ve = m.sb("ve", [P, TT])
        rstd = m.sb("rstd", [P, TT])
        _, bank = m.banks()
        s_apart = m.sem("apart")
        gate_bank = [bank[0:3], bank[3:6]]
        y_bank = [bank[0], bank[1], bank[2], bank[6]]
        ss_bank = bank[7]
        s_const, s_gw, s_X = m.sem("const", "gw", "X")
        s_w = m.sem(*[f"w{i}" for i in range(4)])
        s_whi, s_wlo = m.sem("whi", "wlo")
        s_x, s_xhi, s_xlo = m.sem("x", "xhi", "xlo")
        s_gate, s_sig, s_free = m.sem("gate", "sig", "free")
        s_o, s_og, s_ohi, s_olo, s_acc = m.sem("o", "og", "ohi", "olo", "acc")
        s_proj, s_y, s_ss, s_z, s_ms, s_r, s_ve, s_rstd = m.sem("proj", "y", "ss", "z", "ms", "r", "ve", "rstd")
        s_dve, s_pool = m.sem("dve", "pool")
        block = stack.enter_context(nc.Block())
        order = ["L0_attn_Wi", "L0_attn_Wf", "L0_attn_Wg", "L0_attn_Wo"]

        @block.sync
        def _(sp):
            def load_w(i):
                sp.dma_start(w_raw[i % 2][:], d[order[i]].rearrange("(k p) n -> p k n", p=P)).then_inc(s_w[i], 16)

            def load_x(b):
                src = d["xT"][:, bass.ds(b * T, T)].rearrange("(k p) n -> p k n", p=P)
                sp.dma_start(x_raw[:], src).then_inc(s_x, 16)

            load_w(0)
            load_x(0)
            load_w(1)
            sp.dma_start(gw[:], d["gnorm"]).then_inc(s_gw, 16)
            sp.dma_start(X[:], d["x"].rearrange("(t p) n -> p t n", p=P)).then_inc(s_X, 16)
            for i in (2, 3):
                sp.wait_ge(s_wlo, i - 1)
                load_w(i)
            with sp.Fori(1, B) as b:
                sp.wait_ge(s_xlo, b)
                load_x(b)

        @block.gpsimd
        def _(pool):
            pool.memset(half[:], -0.5).then_inc(s_const, 1)
            pool.wait_ge(s_const, 2)
            with pool.Fori(0, B) as b:
                own = Count(pool, s_pool, b * (KC - 1))
                for t in range(KC):
                    pool.wait_ge(s_o, b * KC + t + 1)
                    if t == 0:
                        pool.wait_ge(s_ss, b + 1)
                        pool.tensor_tensor(sumsq[:, 0, :], o[:, 0, :], o[:, 0, :], ALU.mult).then_inc(s_acc, 1)
                    else:
                        pool.wait_ge(s_acc, b * KC + t)
                        own.done(pool.tensor_tensor(osq[:], o[:, t % 2, :], o[:, t % 2, :], ALU.mult))
                        own.wait()
                        pool.tensor_tensor(sumsq[:, t % 2, :], sumsq[:, (t - 1) % 2, :], osq[:], ALU.add).then_inc(s_acc, 1)
                pool.wait_ge(s_ms, b + 1)
                pool.wait_ge(s_z, b * TT + 1)
                pool.tensor_tensor(rr[:], ms[:], half[:], ALU.pow).then_inc(s_r, 1)
                pool.wait_ge(s_ve, b + 1)
                pool.tensor_tensor(rstd[:], ve[:], half[:], ALU.pow).then_inc(s_rstd, 1)

        @block.scalar
        def _(act):
            def split_hi(i):
                act.wait_ge(s_w[i], 16)
                act.activation(w_hi[i][:], w_raw[i % 2][:], ACT.Copy).then_inc(s_whi, 1)

            def x_split(b):
                act.wait_ge(s_x, b * 16 + 16)
                act.activation(x_hi[:], x_raw[:], ACT.Copy).then_inc(s_xhi, 1)

            split_hi(0)
            x_split(0)
            for i in (1, 2, 3):
                split_hi(i)
            with act.Fori(0, B) as b:
                for t in range(KC):
                    n = b * KC + t
                    for j, (g, s) in enumerate(((0, 1.0), (1, 1.0), (1, -1.0), (2, 1.0))):
                        act.wait_ge(s_gate, n * 3 + g + 1)
                        act.wait_ge(s_free, n + 1)
                        act.activation(sig[:, t % 2, j, :], gate_bank[t % 2][g][:], ACT.Sigmoid, scale=s).then_inc(s_sig, 1)
                    act.wait_ge(s_og, n + 1)
                    act.wait_ge(s_proj, b + 1)
                    act.activation(o_hi[:, t, :], og[:, t % 2, :], ACT.Copy).then_inc(s_ohi, 1)
                with act.If(b < B - 1):
                    act.wait_ge(s_gate, (b * KC + KC) * 3)
                    x_split(b + 1)

        @block.vector
        def _(dve):
            dve.memset(ones[:], 1.0).then_inc(s_const, 1)
            dve.sem_inc(s_free, 2)
            dve.sem_inc(s_z, 1)
            dve.wait_ge(s_gw, 16)

            def split_lo(i):
                dve.wait_ge(s_whi, i + 1)
                dve.tensor_tensor(w_lo[i][:], w_raw[i % 2][:], w_hi[i][:], ALU.subtract).then_inc(s_wlo, 1)

            def x_split(b):
                dve.wait_ge(s_xhi, b + 1)
                dve.tensor_tensor(x_lo[:], x_raw[:], x_hi[:], ALU.subtract).then_inc(s_xlo, 1)

            split_lo(0)
            x_split(0)
            for i in (1, 2, 3):
                split_lo(i)
            dve.wait_ge(s_X, 16)
            per = 2 * KC + 3 * TT
            with dve.Fori(0, B) as b:
                own = Count(dve, s_dve, b * per)
                for t in range(KC):
                    n, q = b * KC + t, t % 2
                    gi, _, gg = gate_bank[q]
                    dve.wait_ge(s_sig, n * 4 + 1)
                    own.done(dve.tensor_tensor(v[:], gi[:], sig[:, q, 0, :], ALU.mult))
                    own.wait()
                    dve.wait_ge(s_sig, n * 4 + 3)
                    own.done(dve.tensor_tensor(v[:], v[:], sig[:, q, 2, :], ALU.mult))
                    own.wait()
                    if t >= 2:
                        dve.wait_ge(s_acc, n - 1)
                    dve.tensor_tensor_scan(o[:, q, :], sig[:, q, 1, :], v[:], 0.0, ALU.mult, ALU.add).then_inc(s_o, 1)
                    dve.wait_ge(s_sig, n * 4 + 4)
                    dve.tensor_tensor(sg[:], gg[:], sig[:, q, 3, :], ALU.mult).then_inc(s_free, 1)
                    dve.wait_ge(s_o, n + 1)
                    dve.wait_ge(s_free, n + 3)
                    dve.scalar_tensor_tensor(og[:, q, :], o[:, q, :], gw[:, t:t + 1], sg[:], ALU.mult, ALU.mult).then_inc(s_og, 1)
                    dve.wait_ge(s_ohi, n + 1)
                    dve.tensor_tensor(o_lo[:, t, :], og[:, q, :], o_hi[:, t, :], ALU.subtract).then_inc(s_olo, 1)
                with dve.If(b < B - 1):
                    x_split(b + 1)
                dve.wait_ge(s_ss, b + 2)
                dve.tensor_scalar(ms[:], ss_bank[:, 0:TT], 1.0 / H, 1e-5, ALU.mult, ALU.add).then_inc(s_ms, 1)
                dve.wait_ge(s_r, b + 1)
                for t in range(TT):
                    xt = one(X[:, bass.ds(b * TT + t, 1), :])
                    dve.wait_ge(s_y, b * TT + t + 1)
                    dve.scalar_tensor_tensor(xt, y_bank[t], rr[:, t:t + 1], xt, ALU.mult, ALU.add).then_inc(s_z, 1)
                apart(dve, s_z, b * TT + TT + 1, s_apart)
                layernorm(dve, X, lambda t: b * TT + t, stats, mv, ve, rstd, own, s_ve, s_rstd, s_apart, b)
                assert own.n == per, own.n

        @block.tensor
        def _(pe):
            pe.sem_inc(s_ss, 1)
            pe.sem_inc(s_proj, 1)
            pe.wait_ge(s_const, 2)
            with pe.Fori(0, B) as b:
                pe.wait_ge(s_xlo, b + 1)
                for t in range(KC):
                    n = b * KC + t
                    pe.wait_ge(s_free, n + 1)
                    if t == 0:
                        pe.wait_ge(s_z, b * TT + 1)
                    for g in range(3):
                        if t == 0:
                            pe.wait_ge(s_wlo, g + 1)
                        product3(pe, gate_bank[t % 2][g][:],
                                 lambda c: w_hi[g][:, c, t * P:(t + 1) * P], lambda c: w_lo[g][:, c, t * P:(t + 1) * P],
                                 lambda c: x_hi[:, c, :], lambda c: x_lo[:, c, :], KC).then_inc(s_gate, 1)
                pe.wait_ge(s_olo, b * KC + KC)
                pe.wait_ge(s_wlo, 4)
                pe.wait_ge(s_free, b * KC + KC + 1)
                pe.wait_ge(s_acc, b * KC + KC)
                for t in range(TT):
                    last = pe.matmul(ss_bank[:, t:t + 1], sumsq[:, 1, t * P:(t + 1) * P], ones[:], start=t == 0, stop=True, skip_group_check=True)
                last.then_inc(s_ss, 1)
                for t in range(TT):
                    ts = slice(t * P, (t + 1) * P)
                    last = product3(pe, y_bank[t][:], lambda c: o_hi[:, c, ts], lambda c: o_lo[:, c, ts],
                                    lambda c: w_hi[3][:, c, :], lambda c: w_lo[3][:, c, :], KC)
                    last.then_inc(s_y, 1)
                pe.wait_ge(s_y, b * TT + TT)
                pe.sem_inc(s_proj, 1)


def queries(nc, X, Qn, ident, d):
    with ExitStack() as stack:
        m = Memory(nc, stack, "q_")
        w_raw = m.sb("w_raw", [P, KC, H])
        w_hi = m.sb("w_hi", [P, KC, H], F32R)
        w_lo = m.sb("w_lo", [P, KC, H], F32R)
        xs = m.sb("xs", [P, TT, H])
        x_hi = m.sb("x_hi", [P, KC, T], F32R)
        x_lo = m.sb("x_lo", [P, KC, T], F32R)
        sq = m.sb("sq", [P, 2, H])
        red = m.sb("red", [P, XH])
        ms = m.sb("ms", [P, 2, XH])
        rr = m.sb("rr", [P, 2, XH])
        half = m.sb("half", [P, XH])
        _, bank = m.banks()
        s_apart = m.sem("apart")
        s_w, s_whi, s_wlo, s_const = m.sem("w", "whi", "wlo", "const")
        s_xs, s_T, s_hi, s_lo, s_q = m.sem("xs", "T", "hi", "lo", "q")
        s_sq, s_ms, s_r, s_qn, s_dve = m.sem("sq", "ms", "r", "qn", "dve")
        block = stack.enter_context(nc.Block())

        @block.sync
        def _(sp):
            sp.dma_start(w_raw[:], d["WqT"].rearrange("(k p) n -> p k n", p=P)).then_inc(s_w, 16)

        @block.gpsimd
        def _(pool):
            pool.memset(half[:], -0.5).then_inc(s_const, 1)
            pool.wait_ge(s_const, 1)
            with pool.Fori(0, B) as b:
                for t in range(TT):
                    n = b * TT + t
                    pool.wait_ge(s_ms, n + 3)
                    pool.wait_ge(s_qn, n + 1)
                    pool.tensor_tensor(rr[:, t % 2, :], ms[:, t % 2, :], half[:], ALU.pow).then_inc(s_r, 1)

        @block.scalar
        def _(act):
            act.wait_ge(s_w, 16)
            act.activation(w_hi[:], w_raw[:], ACT.Copy).then_inc(s_whi, 1)
            with act.Fori(0, B) as b:
                apart(act, s_T, b * KC + KC, s_apart)
                act.activation(xs[:], X[:, bass.ds(b * TT, TT), :], ACT.Copy).then_inc(s_xs, 1)
                act.wait_ge(s_q, b * TT + TT)
                for k in range(KC):
                    act.wait_ge(s_T, b * KC + k + 1 + KC)
                    act.activation(x_hi[:, k, :], bank[k][:], ACT.Copy).then_inc(s_hi, 1)
                for t in range(TT):
                    n = b * TT + t
                    act.wait_ge(s_q, n + 1 + TT)
                    act.wait_ge(s_ms, n + 1)
                    act.activation(sq[:, t % 2, :], bank[4 + t % 2][:], ACT.Square).then_inc(s_sq, 1)

        @block.vector
        def _(dve):
            dve.sem_inc(s_qn, 2)
            dve.sem_inc(s_lo, KC)
            dve.sem_inc(s_ms, 2)
            dve.wait_ge(s_whi, 1)
            dve.tensor_tensor(w_lo[:], w_raw[:], w_hi[:], ALU.subtract).then_inc(s_wlo, 1)
            with dve.Fori(0, B) as b:
                own = Count(dve, s_dve, b * TT)
                for k in range(KC):
                    dve.wait_ge(s_hi, b * KC + k + 1)
                    dve.tensor_tensor(x_lo[:, k, :], bank[k][:], x_hi[:, k, :], ALU.subtract).then_inc(s_lo, 1)

                def normalise(t):
                    dve.wait_ge(s_r, b * TT + t + 1)
                    src = bank[4 + t % 2][:].rearrange("p (h e) -> p h e", e=XD)
                    dst = one(Qn[:, bass.ds(b * TT + t, 1), :]).rearrange("p (h e) -> p h e", e=XD)
                    dve.tensor_tensor(dst, src, rr[:, t % 2, :].unsqueeze(2).to_broadcast([P, XH, XD]), ALU.mult).then_inc(s_qn, 1)

                for t in range(TT):
                    dve.wait_ge(s_sq, b * TT + t + 1)
                    own.done(dve.tensor_reduce(red[:], sq[:, t % 2, :].rearrange("p (h e) -> p h e", e=XD), AX_X, ALU.add))
                    own.wait()
                    dve.tensor_scalar(ms[:, t % 2, :], red[:], 1.0 / XD, 1e-6, ALU.mult, ALU.add).then_inc(s_ms, 1)
                    dve.wait_ge(s_ms, b * TT + t + 3)
                    if t:
                        normalise(t - 1)
                normalise(TT - 1)

        @block.tensor
        def _(pe):
            pe.sem_inc(s_T, KC)
            pe.sem_inc(s_q, TT)
            pe.wait_ge(s_wlo, 1)
            with pe.Fori(0, B) as b:
                pe.wait_ge(s_xs, b + 1)
                for k in range(KC):
                    pe.wait_ge(s_lo, b * KC + k + 1)
                    for t in range(TT):
                        tr = pe.transpose(bank[k][:, t * P:(t + 1) * P], xs[:, t, k * P:(k + 1) * P], ident[:])
                    tr.then_inc(s_T, 1)
                pe.wait_ge(s_lo, b * KC + 2 * KC)
                for t in range(TT):
                    ts = slice(t * P, (t + 1) * P)
                    pe.wait_ge(s_qn, b * TT + t + 1)
                    product3(pe, bank[4 + t % 2][:], lambda c: x_hi[:, c, ts], lambda c: x_lo[:, c, ts],
                             lambda c: w_hi[:, c, :], lambda c: w_lo[:, c, :], KC).then_inc(s_q, 1)


def cross_attention(nc, X, Qn, ident, ident16, d):
    HW = HH * XD
    JOBS = TT + CT
    UNITS = 2 * CT
    with ExitStack() as stack:
        m = Memory(nc, stack, "c_")
        w_hi = m.sb("w_hi", [P, KC, 2 * HW], F32R)
        w_lo = m.sb("w_lo", [P, KC, 2 * HW], F32R)
        c_hi = m.sb("c_hi", [P, 2, KC, P], F32R)
        c_lo = m.sb("c_lo", [P, 2, KC, P], F32R)
        prob = m.sb("prob", [P, 2, HG, T])
        w_raw = prob[:, 1]
        c_raw = prob[:, 0, 0:2, :].rearrange("p s (k t) -> p s k t", k=KC)
        sq = m.sb("sq", [P, HW])
        red = m.sb("red", [P, HH])
        ms = m.sb("ms", [P, 2, HH])
        rr = m.sb("rr", [P, 2, HH])
        half = m.sb("half", [P, HH])
        kn = m.sb("kn", [P, 2, HW])
        rest = m.sb("rest", [P, 2, HW])
        parts = m.sb("parts", [P, 2, HH, 6, XD], BF16)
        qT = m.sb("qT", [SPLIT_ROWS, HH, T], BF16)
        kT = m.sb("kT", [SPLIT_ROWS, HH, CT * P], BF16)
        vx = m.sb("vx", [P, CT, HH, XD + 1])
        oT = m.sb("oT", [P, T])
        rec = m.sb("rec", [P, TT * HG])
        on = m.sb("on", [P, TT, HG, XD])
        half4 = m.sb("half4", [P, TT])
        stats = m.sb("stats", [P, TT, 6])
        mv = m.sb("mv", [P, TT, 2])
        ve = m.sb("ve", [P, TT])
        rstd = m.sb("rstd", [P, TT])
        psum, bank = m.banks()
        s_apart = m.sem("apart")
        kv_bank = bank[0:3]
        tr_bank = [(bank[3], bank[4]), (bank[5], bank[7])]
        score_banks = [psum[:, 2 * i:2 * i + 2, :] for i in range(3)]
        o_bank, ot_bank = bank[6], bank[7]
        s_const, s_ones, s_w, s_whi, s_wlo = m.sem("const", "ones", "w", "whi", "wlo")
        s_c = m.sem("c0", "c1")
        s_hi, s_lo, s_kv, s_sq, s_V, s_ms, s_r, s_kn = m.sem("hi", "lo", "kv", "sq", "V", "ms", "r", "kn")
        s_H, s_R, s_M, s_L, s_tr, s_ev = m.sem("H", "R", "M", "L", "tr", "ev")
        s_sc, s_ex, s_pv, s_oc, s_ot, s_xo = m.sem("sc", "ex", "pv", "oc", "ot", "xo")
        s_ve, s_rstd, s_own, s_red = m.sem("ve", "rstd", "own", "red")
        block = stack.enter_context(nc.Block())
        n_slot = [(CT + 1) // 2, CT // 2]

        def nested(eng, body, after=None):
            with eng.Fori(0, B) as b:
                with eng.Fori(0, 2) as hf:
                    body(b, hf, b * 2 + hf)
                if after:
                    after(b)

        def slots(t4, which, job):
            q = {"H": (0, 3, 1), "M": (3, 5, 1), "L": (5, 6, 1)}
            k = {"H": (1, 6, 2), "M": (2, 5, 2), "L": (0, 1, 1)}
            a, z, s = (q if job < TT else k)[which]
            return t4[:, job % 2, :, a:z:s, :]

        def source(job, b, hf):
            if job < TT:
                ap = one(Qn[:, bass.ds(b * TT + job, 1), bass.ds(hf * HW, HW)])
            else:
                ap = kn[:, job % 2, :]
            return ap.rearrange("p (h e) -> p h e", e=XD)

        @block.sync
        def _(sp):
            def body(b, hf, it):
                sp.wait_ge(s_pv, it * NG * CT + 1)
                sp.dma_start(w_raw, d["WkvT"][bass.ds(hf, 1)].rearrange("o (k p) n -> p (o k) n", p=P)).then_inc(s_w, 16)
                for n in range(CT):
                    if n >= 2:
                        sp.wait_ge(s_lo, it * CT + n - 1)
                    sp.dma_start(c_raw[:, n % 2], d["ctxT"][bass.ds(b, 1), n].rearrange("o p (k t) -> p (o k) t", k=KC)
                                 ).then_inc(s_c[n % 2], 16)
            nested(sp, body)

        @block.gpsimd
        def _(pool):
            pool.memset(half[:], -0.5).then_inc(s_const, 1)
            pool.memset(half4[:], -0.5).then_inc(s_const, 1)
            pool.wait_ge(s_const, 2)

            def body(b, hf, it):
                for n in range(CT):
                    pool.wait_ge(s_ms, it * CT + n + 1)
                    if n >= 2:
                        pool.wait_ge(s_kn, it * CT + n - 1)
                    pool.tensor_tensor(rr[:, n % 2, :], ms[:, n % 2, :], half[:], ALU.pow).then_inc(s_r, 1)

            def after(b):
                pool.wait_ge(s_ve, b + 1)
                pool.tensor_tensor(rstd[:], ve[:], half4[:], ALU.pow).then_inc(s_rstd, 1)
            nested(pool, body, after)

        @block.scalar
        def _(act):
            def body(b, hf, it):
                act.wait_ge(s_w, it * 16 + 16)
                act.wait_ge(s_pv, it * NG * CT + 1)
                act.activation(w_hi[:], w_raw, ACT.Copy).then_inc(s_whi, 1)
                for s in range(JOBS + 5):
                    if 0 <= (j := s - 3) < JOBS:
                        if j >= TT:
                            act.wait_ge(s_kn, it * CT + j - TT + 1)
                        if j >= 2:
                            act.wait_ge(s_tr, it * JOBS + j - 1)
                        act.activation(slots(parts, "H", j), source(j, b, hf).unsqueeze(2).to_broadcast([P, HH, 3, XD]), ACT.Copy).then_inc(s_H, 1)
                    if 0 <= (j := s - 4) < JOBS:
                        act.wait_ge(s_R, it * JOBS + j + 1)
                        act.activation(slots(parts, "M", j), rest[:, j % 2, :].rearrange("p (h e) -> p h e", e=XD).unsqueeze(2).to_broadcast([P, HH, 2, XD]), ACT.Copy).then_inc(s_M, 1)
                    if 0 <= (n := s - TT) < CT:
                        act.wait_ge(s_c[n % 2], (it * n_slot[n % 2] + n // 2) * 16 + 16)
                        if n >= 2:
                            act.wait_ge(s_kv, it * CT + n - 1)
                        act.activation(c_hi[:, n % 2], c_raw[:, n % 2], ACT.Copy).then_inc(s_hi, 1)
                    if 0 <= (n := s - TT - 1) < CT:
                        act.wait_ge(s_kv, it * CT + n + 1)
                        if n >= 1:
                            act.wait_ge(s_red, it * CT + n)
                        act.activation(sq[:], kv_bank[n % 3][:, 0:HW], ACT.Square).then_inc(s_sq, 1)
                        act.activation(vx[:, n, :, 0:XD], kv_bank[n % 3][:, HW:2 * HW].rearrange("p (h e) -> p h e", e=XD), ACT.Copy).then_inc(s_V, 1)
                for g in range(NG):
                    for u in range(UNITS):
                        lu = g * UNITS + u
                        kt, lt = u // 2, g * CT + u // 2
                        act.wait_ge(s_sc, it * NG * UNITS + lu + 1)
                        if lt >= 2 and u % 2 == 0:
                            act.wait_ge(s_pv, it * NG * CT + lt)
                        act.activation(prob[:, lt % 2, 2 * (u % 2):2 * (u % 2) + 2, :], score_banks[lu % 3], ACT.Exp, scale=XD ** -0.5).then_inc(s_ex, 1)
            nested(act, body)

        @block.vector
        def _(dve):
            dve.memset(o_bank[:], 0.0).then_inc(s_ones, 1)
            dve.memset(vx[:, 0:CT - 1, :, XD:XD + 1], 1.0).then_inc(s_ones, 1)
            dve.memset(vx[:, CT - 1, :, XD:XD + 1], 0.0).then_inc(s_ones, 1)
            dve.wait_ge(s_ones, 3)
            dve.memset(vx[0:LAST, CT - 1, :, XD:XD + 1], 1.0).then_inc(s_ones, 1)
            dve.sem_inc(s_oc, 1)
            dve.sem_inc(s_xo, 1)

            def body(b, hf, it):
                own = Count(dve, s_own, it * 2 * NG + b * 3 * TT)
                dve.wait_ge(s_whi, it + 1)
                dve.tensor_tensor(w_lo[:], w_raw, w_hi[:], ALU.subtract).then_inc(s_wlo, 1)
                for s in range(JOBS + 6):
                    if 0 <= (n := s - TT - 2) < CT:
                        j = n + TT
                        dve.wait_ge(s_r, it * CT + n + 1)
                        dve.wait_ge(s_V, it * CT + n + 1)
                        if n >= 2:
                            dve.wait_ge(s_H, it * JOBS + j - 1)
                        dve.tensor_tensor(kn[:, j % 2, :].rearrange("p (h e) -> p h e", e=XD),
                                          kv_bank[n % 3][:, 0:HW].rearrange("p (h e) -> p h e", e=XD),
                                          rr[:, n % 2, :].unsqueeze(2).to_broadcast([P, HH, XD]), ALU.mult).then_inc(s_kn, 1)
                    if 0 <= (j := s - 3) < JOBS:
                        dve.wait_ge(s_H, it * JOBS + j + 1)
                        if j >= TT:
                            dve.wait_ge(s_kn, it * CT + j - TT + 1)
                        if j >= 2:
                            dve.wait_ge(s_L, it * JOBS + j - 1)
                        h0 = slots(parts, "H", j)[:, :, 0, :]
                        dve.tensor_tensor(rest[:, j % 2, :].rearrange("p (h e) -> p h e", e=XD), source(j, b, hf), h0, ALU.subtract).then_inc(s_R, 1)
                    if 0 <= (j := s - 4) < JOBS:
                        dve.wait_ge(s_M, it * JOBS + j + 1)
                        dve.wait_ge(s_R, it * JOBS + j + 1)
                        m0 = slots(parts, "M", j)[:, :, 0, :]
                        dve.tensor_tensor(slots(parts, "L", j)[:, :, 0, :], rest[:, j % 2, :].rearrange("p (h e) -> p h e", e=XD), m0, ALU.subtract).then_inc(s_L, 1)
                    if 0 <= (n := s - TT) < CT:
                        dve.wait_ge(s_hi, it * CT + n + 1)
                        dve.tensor_tensor(c_lo[:, n % 2], c_raw[:, n % 2], c_hi[:, n % 2], ALU.subtract).then_inc(s_lo, 1)
                    if 0 <= (n := s - TT - 1) < CT:
                        dve.wait_ge(s_sq, it * CT + n + 1)
                        dve.tensor_reduce(red[:], sq[:].rearrange("p (h e) -> p h e", e=XD), AX_X, ALU.add).then_inc(s_red, 1)
                        dve.wait_ge(s_red, it * CT + n + 1)
                        if n >= 2:
                            dve.wait_ge(s_r, it * CT + n - 1)
                        dve.tensor_scalar(ms[:, n % 2, :], red[:], 1.0 / XD, 1e-6, ALU.mult, ALU.add).then_inc(s_ms, 1)
                        dve.wait_ge(s_ms, it * CT + n + 1)
                    if 0 <= (j := s - 5) < JOBS:
                        dve.wait_ge(s_tr, it * JOBS + j + 1)
                        for i in range(2):
                            src = tr_bank[j % 2][i][:].bitcast(BF16)[0:SPLIT_ROWS, :].rearrange("p (h t) -> p h t", t=P)
                            dst = qT[:, 8 * i:8 * i + 8, j * P:(j + 1) * P] if j < TT else kT[:, 8 * i:8 * i + 8, (j - TT) * P:(j - TT + 1) * P]
                            dve.tensor_copy(dst, src).then_inc(s_ev, 1)
                for g in range(NG):
                    gi = it * NG + g
                    dve.wait_ge(s_pv, gi * CT + CT + 1)
                    dve.tensor_copy(oT[:], o_bank[:]).then_inc(s_oc, 1)
                    dve.wait_ge(s_ot, gi + 1)
                    ot = ot_bank[:].rearrange("p (t g e) -> p t g e", t=TT, g=HG)
                    own.done(dve.reciprocal(rec[:].rearrange("p (t g) -> p t g", t=TT), ot[:, :, :, XD]))
                    own.wait()
                    own.done(dve.tensor_tensor(on[:].rearrange("p t g e -> p (t g) e"), ot_bank[:].rearrange("p (q e) -> p q e", e=32)[:, :, 0:XD],
                                               rec[:].unsqueeze(2).to_broadcast([P, TT * HG, XD]), ALU.mult))
                    own.wait()
                    xo = X[:, bass.ds(b * TT, TT), bass.ds(hf * HW + g * HG * XD, HG * XD)]
                    dve.tensor_tensor(xo, xo, on[:].rearrange("p t g e -> p t (g e)"), ALU.add).then_inc(s_xo, 1)
                    dve.wait_ge(s_xo, gi + 2)

            def after(b):
                own = Count(dve, s_own, (b * 2 + 2) * 2 * NG + b * 3 * TT)
                layernorm(dve, X, lambda t: b * TT + t, stats, mv, ve, rstd, own, s_ve, s_rstd, s_apart, b)
            nested(dve, body, after)

        @block.tensor
        def _(pe):
            pe.sem_inc(s_pv, 1)
            pe.wait_ge(s_ones, 4)

            def body(b, hf, it):
                pe.wait_ge(s_wlo, it + 1)
                for s in range(JOBS + 5):
                    if 0 <= (n := s - TT) < CT:
                        pe.wait_ge(s_lo, it * CT + n + 1)
                        if n >= 3:
                            pe.wait_ge(s_kn, it * CT + n - 2)
                            pe.wait_ge(s_V, it * CT + n - 2)
                        product3(pe, kv_bank[n % 3][:], lambda c: c_hi[:, n % 2, c, :], lambda c: c_lo[:, n % 2, c, :],
                                 lambda c: w_hi[:, c, :], lambda c: w_lo[:, c, :], KC).then_inc(s_kv, 1)
                    if 0 <= (j := s - 4) < JOBS:
                        pe.wait_ge(s_L, it * JOBS + j + 1)
                        if j >= 2:
                            pe.wait_ge(s_ev, (it * JOBS + j - 1) * 2)
                        for h in range(HH):
                            out = tr_bank[j % 2][h // 8][:].bitcast(BF16)[0:SPLIT_ROWS, (h % 8) * P:(h % 8 + 1) * P]
                            tr = pe.transpose(out, parts[:, j % 2, h].rearrange("p r e -> p (r e)"), ident16[:])
                        tr.then_inc(s_tr, 1)
                pe.wait_ge(s_ev, (it * JOBS + JOBS) * 2)
                pe.wait_ge(s_V, it * CT + CT)

                def scores(g, u):
                    lu = g * UNITS + u
                    if lu >= 3:
                        pe.wait_ge(s_ex, it * NG * UNITS + lu - 2)
                    for j in range(2):
                        h = g * HG + 2 * (u % 2) + j
                        mm = pe.matmul(score_banks[lu % 3][:, j, :], kT[:, h, (u // 2) * P:(u // 2 + 1) * P], qT[:, h, :], start=True, stop=True)
                    mm.then_inc(s_sc, 1)

                def turn(g):
                    gi = it * NG + g
                    pe.wait_ge(s_oc, gi + 2)
                    pe.wait_ge(s_xo, gi + 1)
                    for t in range(TT):
                        tr = pe.transpose(ot_bank[:, t * P:(t + 1) * P], oT[:, t * P:(t + 1) * P], ident[:])
                    tr.then_inc(s_ot, 1)

                for u in range(3):
                    scores(0, u)
                for lt in range(NG * CT):
                    g, kt = divmod(lt, CT)
                    for u in (2 * lt + 3, 2 * lt + 4):
                        if u < NG * UNITS:
                            scores(*divmod(u, UNITS))
                    pe.wait_ge(s_ex, it * NG * UNITS + 2 * lt + 2)
                    if kt == 0:
                        pe.wait_ge(s_oc, it * NG + g + 1)
                    for j in range(HG):
                        mm = pe.matmul(o_bank[32 * j:32 * j + XD + 1, :], vx[:, kt, g * HG + j, :], prob[:, lt % 2, j, :],
                                       start=kt == 0, stop=kt == CT - 1)
                    mm.then_inc(s_pv, 1)
                    if kt == 2 and g:
                        turn(g - 1)
                turn(NG - 1)
            nested(pe, body)


def self_attention(nc, X, x0, ident, ident16, d):
    HPC = P // SD
    UNITS = KC * HPC * TT
    SCALE = SD ** -0.5
    BLOCKS = TT * (TT + 1) // 2
    with ExitStack() as stack:
        m = Memory(nc, stack, "s_")
        names = ["wq", "wk", "wv", "wo"]
        w_hi = [m.sb(f"w_hi{i}", [P, KC, H], F32R) for i in range(4)]
        w_lo = [m.sb(f"w_lo{i}", [P, KC, H], F32R) for i in range(4)]
        w1 = m.sb("w1", [P, KC])
        bqk = m.sb("bqk", [P, 2, KC])
        bv = m.sb("bv", [P, H])
        cos = m.sb("cos", [P, T])
        sin = m.sb("sin", [P, T])
        h_hi = m.sb("h_hi", [P, KC, T], F32R)
        h_lo = m.sb("h_lo", [P, KC, T], F32R)
        v = m.sb("v", [P, TT, H])
        qk = m.sb("qk", [P, 2, T])
        turned = m.sb("turned", [P, T])
        tcos = m.sb("tcos", [P, T])
        rot = m.sb("rot", [P, 2, T])
        q_hi = m.sb("q_hi", [P, 2, T], F32R)
        q_lo = m.sb("q_lo", [P, 2, T], F32R)
        k_hi = m.sb("k_hi", [P, HPC, T], F32R)
        k_lo = m.sb("k_lo", [P, HPC, T], F32R)
        p = m.sb("p", [P, 3, T])
        pT = m.sb("pT", [P, HPC, BLOCKS * P])
        xs = pT[:, 0:2, :].rearrange("p a n -> p (a n)")[:, 0:TT * H].rearrange("p (t n) -> p t n", t=TT)
        w_raw = pT[:, 2:4, :].rearrange("p a n -> p (a n)")[:, 0:KC * H].rearrange("p (k n) -> p k n", k=KC)
        a_hi = m.sb("a_hi", [P, KC, T], F32R)
        a_lo = m.sb("a_lo", [P, KC, T], F32R)
        neg = m.sb("neg", [P, P], BF16)
        half = m.sb("half", [P, TT])
        ss = m.sb("ss", [P, TT])
        ms = m.sb("ms", [P, TT])
        rr = m.sb("rr", [P, TT])
        top = m.sb("top", [P, 2])
        bias = m.sb("bias", [P, 3])
        rs = m.sb("rs", [P, 3])
        rc = m.sb("rc", [P, 2])
        psum, bank = m.banks()
        s_apart = m.sem("apart")
        h_bank, sc_bank, tr_bank, o_bank, y_bank = bank[0:4], bank[0:3], bank[3:5], bank[5], bank[6:8]
        s_const, s_zero, s_ld, s_saved = m.sem("const", "zero", "ld", "saved")
        s_w = m.sem(*[f"w{i}" for i in range(4)])
        s_whi, s_wlo = m.sem("whi", "wlo")
        s_ss, s_ms, s_r, s_xs, s_T, s_hhi, s_hlo = m.sem("ss", "ms", "r", "xs", "T", "hhi", "hlo")
        s_v, s_vs, s_qk, s_qb, s_tc, s_rot, s_own = m.sem("v", "vs", "qk", "qb", "tc", "rot", "own")
        s_qhi, s_qlo, s_khi, s_klo = m.sem("qhi", "qlo", "khi", "klo")
        s_sc, s_nb, s_ex, s_pn, s_tr, s_ev, s_top, s_rc = m.sem("sc", "nb", "ex", "pn", "tr", "ev", "top", "rc")
        s_o, s_ahi, s_alo, s_y, s_x = m.sem("o", "ahi", "alo", "y", "x")
        block = stack.enter_context(nc.Block())

        QK, KPREP, QPREP = 0, (8, 10, 13, 15), 11

        def chunk_events(n):
            c, r = divmod(n, HPC * TT)
            if c + 1 == KC:
                return []
            got = [(c + 1, "qk")] if r == QK else []
            got += [(c + 1, "q")] if r == QPREP else []
            return got + [(c + 1, j) for j in range(HPC) if r == KPREP[j]]

        @block.sync
        def _(sp):
            for dst, src in ((w1, "w1"), (bqk, "bqk"), (bv, "bv"), (cos, "cos"), (sin, "sin")):
                sp.dma_start(dst[:], d[src]).then_inc(s_ld, 16)
            for i in range(4):
                dst = w_raw if i % 2 else xs
                if i >= 2:
                    sp.wait_ge(s_wlo, i - 1)
                sp.dma_start(dst, d[names[i]].rearrange("(k p) n -> p k n", p=P)).then_inc(s_w[i], 16)
            sp.dma_start(x0.rearrange("p (t n) -> p t n", t=B * TT), X[:]).then_inc(s_saved, 16)

        @block.gpsimd
        def _(pool):
            pool.memset(half[:], -0.5).then_inc(s_const, 1)
            pool.memset(neg[:], 0.0).then_inc(s_const, 1)
            pool.wait_ge(s_const, 2)
            pool.affine_select(out=neg[:], in_=neg[:], compare_op=ALU.is_ge, fill=-1e30, base=0,
                               pattern=[[-1, P]], channel_multiplier=1).then_inc(s_const, 1)
            pool.wait_ge(s_ld, 80)
            with pool.Fori(0, B) as b:
                pool.wait_ge(s_ms, b + 1)
                pool.tensor_tensor(rr[:], ms[:], half[:], ALU.pow).then_inc(s_r, 1)
                for i in range(2 * KC):
                    pool.wait_ge(s_qb, b * 2 * KC + i + 1)
                    pool.wait_ge(s_rot, b * 2 * KC + i + 1)
                    pool.tensor_tensor(tcos[:], qk[:, i % 2, :], cos[:], ALU.mult).then_inc(s_tc, 1)

        @block.scalar
        def _(act):
            for i in range(4):
                act.wait_ge(s_w[i], 16)
                act.activation(w_hi[i][:], w_raw if i % 2 else xs, ACT.Copy).then_inc(s_whi, 1)
            act.wait_ge(s_ld, 80)
            act.wait_ge(s_wlo, 4)
            act.wait_ge(s_zero, 2)

            with act.Fori(0, B) as b:
                for t in range(TT):
                    act.activation(xs[:, t, :], one(X[:, bass.ds(b * TT + t, 1), :]), ACT.Square, accum_out=ss[:, t:t + 1]).then_inc(s_ss, 1)
                apart(act, s_r, b + 1, s_apart)
                for t in range(TT):
                    act.activation(xs[:, t, :], one(X[:, bass.ds(b * TT + t, 1), :]), ACT.Copy, scale=rr[:, t:t + 1]).then_inc(s_xs, 1)
                for k in range(KC):
                    act.wait_ge(s_T, b * KC + k + 1)
                    act.activation(h_hi[:, k, :], h_bank[k], ACT.Copy, scale=w1[:, k:k + 1]).then_inc(s_hhi, 1)

                def event(c, what):
                    if what == "qk":
                        for i in range(2):
                            n = 2 * c + i
                            act.wait_ge(s_qk, b * 2 * KC + n + 1)
                            if n >= 2:
                                act.wait_ge(s_rot, b * 2 * KC + n)
                            act.activation(qk[:, i, :], y_bank[n % 2], ACT.Identity, bias=bqk[:, i, c:c + 1]).then_inc(s_qb, 1)
                    elif what == "q":
                        act.wait_ge(s_rot, b * 2 * KC + 2 * c + 2)
                        act.activation(q_hi[:, c % 2, :], rot[:, 0, :], ACT.Copy).then_inc(s_qhi, 1)
                    else:
                        r = slice(32 * what, 32 * what + 32)
                        act.wait_ge(s_rot, b * 2 * KC + 2 * c + 3)
                        if c:
                            act.wait_ge(s_sc, b * UNITS + ((c - 1) * HPC + what) * TT + TT)
                        act.activation(k_hi[r, what, :], rot[r, 1, :], ACT.Copy).then_inc(s_khi, 1)

                for e in ("qk", "q", 0, 1, 2, 3):
                    event(0, e)
                for n in range(UNITS + 3):
                    if n < UNITS:
                        t = n % TT
                        L = (t + 1) * P
                        act.wait_ge(s_nb, b * UNITS + n + 1)
                        if n >= 3:
                            act.wait_ge(s_tr, b * UNITS + n - 2)
                        act.activation(p[:, n % 3, 0:L], sc_bank[n % 3][:, 0:L], ACT.Exp, bias=bias[:, n % 3:n % 3 + 1],
                                       scale=SCALE, accum_out=rs[:, n % 3:n % 3 + 1]).then_inc(s_ex, 1)
                        for e in chunk_events(n):
                            event(*e)
                    if 0 <= (u := n - 2) < UNITS:
                        c, j, t = u // (HPC * TT), u // TT % HPC, u % TT
                        act.wait_ge(s_tr, b * UNITS + u + 1)
                        if j == 0 and t == 0 and c:
                            act.wait_ge(s_o, b * KC + c)
                        at = t * (t + 1) // 2 * P
                        act.activation(pT[:, j, at:at + (t + 1) * P], tr_bank[u % 2][:, 0:(t + 1) * P], ACT.Copy).then_inc(s_ev, 1)
                    if 0 <= n - 3 < UNITS and (n - 3) % (HPC * TT) == HPC * TT - 1:
                        c = (n - 3) // (HPC * TT)
                        act.wait_ge(s_o, b * KC + c + 1)
                        act.activation(a_hi[:, c, :], o_bank, ACT.Copy).then_inc(s_ahi, 1)
                act.wait_ge(s_x, b * TT + TT)

        @block.vector
        def _(dve):
            dve.memset(k_hi[:].bitcast(F32), 0.0).then_inc(s_zero, 1)
            dve.memset(k_lo[:].bitcast(F32), 0.0).then_inc(s_zero, 1)
            dve.sem_inc(s_rot, 1)
            for i in range(4):
                dve.wait_ge(s_whi, i + 1)
                dve.tensor_tensor(w_lo[i][:], w_raw if i % 2 else xs, w_hi[i][:], ALU.subtract).then_inc(s_wlo, 1)
            dve.wait_ge(s_ld, 80)
            dve.wait_ge(s_zero, 2)
            dve.wait_ge(s_saved, 16)
            with dve.Fori(0, B) as b:
                own = Count(dve, s_own, b * 4 * KC)
                dve.wait_ge(s_ss, b * TT + TT)
                dve.tensor_scalar(ms[:], ss[:], 1.0 / H, 1e-6, ALU.mult, ALU.add).then_inc(s_ms, 1)
                for k in range(KC):
                    dve.wait_ge(s_hhi, b * KC + k + 1)
                    dve.scalar_tensor_tensor(h_lo[:, k, :], h_bank[k], w1[:, k:k + 1], h_hi[:, k, :], ALU.mult, ALU.subtract).then_inc(s_hlo, 1)
                for t in range(TT):
                    dve.wait_ge(s_v, b * TT + t + 1)
                    dve.tensor_tensor(v[:, t, :], y_bank[t % 2], bv[:], ALU.add).then_inc(s_vs, 1)

                def event(c, what):
                    if what == "qk":
                        for i in range(2):
                            n = b * 2 * KC + 2 * c + i
                            apart(dve, s_qb, n + 1, s_apart)
                            own.done(dve.stream_shuffle(turned[:], qk[:, i, :], [(r + SD // 2) % SD for r in range(SD)]))
                            own.wait()
                            own.done(dve.tensor_tensor(turned[:], turned[:], sin[:], ALU.mult))
                            own.wait()
                            dve.wait_ge(s_tc, n + 1)
                            if c:
                                if i == 0:
                                    dve.wait_ge(s_qlo, b * KC + c)
                                    dve.wait_ge(s_qhi, b * KC + c)
                                else:
                                    dve.wait_ge(s_klo, (b * KC + c) * HPC)
                            dve.tensor_tensor(rot[:, i, :], tcos[:], turned[:], ALU.add).then_inc(s_rot, 1)
                            dve.wait_ge(s_rot, n + 2)
                    elif what == "q":
                        dve.wait_ge(s_qhi, b * KC + c + 1)
                        dve.tensor_tensor(q_lo[:, c % 2, :], rot[:, 0, :], q_hi[:, c % 2, :], ALU.subtract).then_inc(s_qlo, 1)
                    else:
                        r = slice(32 * what, 32 * what + 32)
                        dve.wait_ge(s_khi, (b * KC + c) * HPC + what + 1)
                        dve.tensor_tensor(k_lo[r, what, :], rot[r, 1, :], k_hi[r, what, :], ALU.subtract).then_inc(s_klo, 1)

                for e in ("qk", "q", 0, 1, 2, 3):
                    event(0, e)
                for n in range(UNITS + 4):
                    if n < UNITS:
                        L = (n % TT + 1) * P
                        g = b * UNITS + n
                        dve.wait_ge(s_sc, g + 1)
                        dve.reduce_max(top[:, n % 2:n % 2 + 1], sc_bank[n % 3][:, 0:L], AX_X).then_inc(s_top, 1)
                        dve.wait_ge(s_top, g + 1)
                        if n >= 3:
                            dve.wait_ge(s_ex, g - 2)
                        dve.tensor_scalar(bias[:, n % 3:n % 3 + 1], top[:, n % 2:n % 2 + 1], -SCALE, None, ALU.mult).then_inc(s_nb, 1)
                        for e in chunk_events(n):
                            event(*e)
                    if 0 <= (u := n - 1) < UNITS:
                        L = (u % TT + 1) * P
                        g = b * UNITS + u
                        dve.wait_ge(s_ex, g + 1)
                        if u >= 2:
                            dve.wait_ge(s_pn, g - 1)
                        dve.reciprocal(rc[:, u % 2:u % 2 + 1], rs[:, u % 3:u % 3 + 1]).then_inc(s_rc, 1)
                        dve.wait_ge(s_rc, g + 1)
                        dve.tensor_scalar(p[:, u % 3, 0:L], p[:, u % 3, 0:L], rc[:, u % 2:u % 2 + 1], None, ALU.mult).then_inc(s_pn, 1)
                    if 0 <= n - 3 < UNITS and (n - 3) % (HPC * TT) == HPC * TT - 1:
                        c = (n - 3) // (HPC * TT)
                        dve.wait_ge(s_ahi, b * KC + c + 1)
                        dve.tensor_tensor(a_lo[:, c, :], o_bank, a_hi[:, c, :], ALU.subtract).then_inc(s_alo, 1)
                for t in range(TT):
                    xt = one(X[:, bass.ds(b * TT + t, 1), :])
                    dve.wait_ge(s_y, b * TT + t + 1)
                    dve.tensor_tensor(xt, xt, y_bank[t % 2], ALU.add).then_inc(s_x, 1)

        @block.tensor
        def _(pe):
            pe.wait_ge(s_const, 3)
            pe.wait_ge(s_wlo, 4)
            with pe.Fori(0, B) as b:
                for k in range(KC):
                    for t in range(TT):
                        pe.wait_ge(s_xs, b * TT + t + 1)
                        tr = pe.transpose(h_bank[k][:, t * P:(t + 1) * P], xs[:, t, k * P:(k + 1) * P], ident[:])
                    tr.then_inc(s_T, 1)
                pe.wait_ge(s_hlo, b * KC + KC)
                h = (lambda c: h_hi[:, c, :], lambda c: h_lo[:, c, :])
                for t in range(TT):
                    ts = slice(t * P, (t + 1) * P)
                    if t >= 2:
                        pe.wait_ge(s_vs, b * TT + t - 1)
                    product3(pe, y_bank[t % 2], lambda c: h_hi[:, c, ts], lambda c: h_lo[:, c, ts],
                             lambda c: w_hi[2][:, c, :], lambda c: w_lo[2][:, c, :], KC).then_inc(s_v, 1)

                def project(c):
                    fs = slice(c * P, (c + 1) * P)
                    for i in range(2):
                        if c == 0:
                            pe.wait_ge(s_vs, b * TT + 3 + i)
                        else:
                            pe.wait_ge(s_qb, b * 2 * KC + 2 * (c - 1) + i + 1)
                        product3(pe, y_bank[i], lambda k: w_hi[i][:, k, fs], lambda k: w_lo[i][:, k, fs], *h, KC).then_inc(s_qk, 1)

                def weighted(c):
                    pe.wait_ge(s_ev, b * UNITS + (c + 1) * HPC * TT)
                    if c:
                        pe.wait_ge(s_alo, b * KC + c)
                    for t in range(TT):
                        at = t * (t + 1) // 2
                        for kt in range(t + 1):
                            for j in range(HPC):
                                hd = c * HPC + j
                                mm = pe.matmul(o_bank[32 * j:32 * j + 32, t * P:(t + 1) * P], v[:, kt, hd * SD:(hd + 1) * SD],
                                               pT[:, j, (at + kt) * P:(at + kt + 1) * P], start=kt == 0, stop=kt == t)
                    mm.then_inc(s_o, 1)

                project(0)
                for n in range(UNITS + 3):
                    if n < UNITS:
                        c, j, t = n // (HPC * TT), n // TT % HPC, n % TT
                        L = (t + 1) * P
                        ts = slice(t * P, L)
                        if t == 0:
                            pe.wait_ge(s_klo, (b * KC + c) * HPC + j + 1)
                        if j == 0 and t == 0:
                            pe.wait_ge(s_qlo, b * KC + c + 1)
                        if n >= 3:
                            pe.wait_ge(s_ex, b * UNITS + n - 2)
                        out = sc_bank[n % 3][:, 0:L]
                        pe.matmul(out, q_hi[:, c % 2, ts], k_hi[:, j, 0:L], start=True, stop=False)
                        pe.matmul(out, q_hi[:, c % 2, ts], k_lo[:, j, 0:L], start=False, stop=False)
                        pe.matmul(sc_bank[n % 3][:, ts], ident16[:], neg[:], start=False, stop=False, skip_group_check=True)
                        pe.matmul(out, q_lo[:, c % 2, ts], k_hi[:, j, 0:L], start=False, stop=True).then_inc(s_sc, 1)
                        for e in chunk_events(n):
                            if e[1] == "qk":
                                project(e[0])
                    if 0 <= (u := n - 2) < UNITS:
                        if u and u % (HPC * TT) == 0:
                            weighted(u // (HPC * TT) - 1)
                        pe.wait_ge(s_pn, b * UNITS + u + 1)
                        if u >= 2:
                            pe.wait_ge(s_ev, b * UNITS + u - 1)
                        for kt in range(u % TT + 1):
                            tr = pe.transpose(tr_bank[u % 2][:, kt * P:(kt + 1) * P], p[:, u % 3, kt * P:(kt + 1) * P], ident[:])
                        tr.then_inc(s_tr, 1)
                weighted(KC - 1)
                pe.wait_ge(s_alo, b * KC + KC)
                for t in range(TT):
                    ts = slice(t * P, (t + 1) * P)
                    if t >= 2:
                        pe.wait_ge(s_x, b * TT + t - 1)
                    product3(pe, y_bank[t % 2], lambda c: a_hi[:, c, ts], lambda c: a_lo[:, c, ts],
                             lambda c: w_hi[3][:, c, :], lambda c: w_lo[3][:, c, :], KC).then_inc(s_y, 1)


def moe(nc, X, x0, ident, d, out):
    GU, DN = KC * MI, len(IT) * H
    NR = NEXP + 1
    with ExitStack() as stack:
        m = Memory(nc, stack, "m_")
        h_hi = m.sb("h_hi", [P, KC, B * T], F32R)
        h_lo = m.sb("h_lo", [P, KC, B * T], F32R)
        up_raw = m.sb("up_raw", [P, 2, KC, MI])
        dn_raw = m.sb("dn_raw", [P, len(IT), H])
        up_hi = m.sb("up_hi", [P, 2, 2, KC, MI], F32R)
        up_lo = m.sb("up_lo", [P, 2, 2, KC, MI], F32R)
        dn_hi = m.sb("dn_hi", [P, len(IT), H], F32R)
        dn_lo = m.sb("dn_lo", [P, len(IT), H], F32R)
        a_hi = m.sb("a_hi", [P, 2, len(IT), T], F32R)
        a_lo = m.sb("a_lo", [P, 2, len(IT), T], F32R)
        xs = up_raw[:].rearrange("p a k n -> p (a k n)")[:, 0:TT * H].rearrange("p (t n) -> p t n", t=TT)
        x_in = a_hi[:].bitcast(F32).rearrange("p a i n -> p (a i n)")[:, 0:TT * H].rearrange("p (t n) -> p t n", t=TT)
        sig = m.sb("sig", [P, T])
        rT = sig
        act_f = m.sb("act_f", [P, T])
        w2 = m.sb("w2", [P, KC])
        wr = dn_raw[:].rearrange("p i n -> p (i n)")[:, 0:KC * P].rearrange("p (k n) -> p k n", k=KC)
        wr_hi = m.sb("wr_hi", [P, KC, P], F32R)
        wr_lo = m.sb("wr_lo", [P, KC, P], F32R)
        half = m.sb("half", [P, TT])
        ss = m.sb("ss", [P, TT])
        ms = m.sb("ms", [P, TT])
        rr = m.sb("rr", [P, TT])
        NTILE = B * TT
        logit = m.sb("logit", [P, NTILE, NR])
        prob = m.sb("prob", [P, NTILE, NEXP])
        small = m.sb("small", [P, NTILE])
        rank = m.sb("rank", [P, NTILE, NEXP])
        above = m.sb("above", [P, NTILE, NEXP])
        comb = m.sb("comb", [P, NTILE, NE])
        stats = m.sb("stats", [P, TT, 6])
        mv = m.sb("mv", [P, TT, 2])
        ve = m.sb("ve", [P, TT])
        rstd = m.sb("rstd", [P, TT])
        psum, bank = m.banks()
        s_apart = m.sem("apart")
        h_bank, rT_bank, r_bank = bank[0:4], bank[4], bank[5]
        gu_bank = [(bank[0], bank[1]), (bank[2], bank[3])]
        y_bank = bank[4:8]
        s_const, s_ld, s_wr, s_wrhi = m.sem("const", "ld", "wr", "wrhi")
        s_ss, s_ms, s_r, s_xs, s_T, s_hhi, s_hlo = m.sem("ss", "ms", "r", "xs", "T", "hhi", "hlo")
        s_lg, s_lc, s_own, s_ex, s_mid, s_sg = m.sem("lg", "lc", "own", "ex", "mid", "sg")
        s_up, s_dn, s_uphi, s_uplo, s_dnhi, s_dnlo = m.sem("up", "dn", "uphi", "uplo", "dnhi", "dnlo")
        s_gu, s_sig, s_t1, s_a, s_ahi, s_alo, s_y, s_x = m.sem("gu", "sig", "t1", "a", "ahi", "alo", "y", "x")
        s_ve, s_rstd, s_fin, s_out, s_route, s_own2 = m.sem("ve", "rstd", "fin", "out", "route", "own2")
        s_in, s_add = m.sem("in", "add")
        block = stack.enter_context(nc.Block())
        NI = len(IT)

        @block.sync
        def _(sp):
            sp.dma_start(w2[:], d["w2"]).then_inc(s_ld, 16)
            sp.dma_start(wr, d["wr"].rearrange("(k p) n -> p k n", p=P)).then_inc(s_ld, 16)
            with sp.Fori(0, B) as b:
                sp.wait_ge(s_add, b + 1)
                sp.dma_start(x_in, x0.rearrange("p (t n) -> p t n", t=B * TT)[:, bass.ds(b * TT, TT), :]).then_inc(s_in, 16)
            sp.wait_ge(s_wr, 1)
            sp.wait_ge(s_T, B * KC + KC)
            with sp.Fori(0, NE) as e:
                sp.wait_ge(s_uplo, e + 1)
                sp.dma_start(up_raw[:], d["up"][bass.ds(e, 1)].rearrange("o p n -> p (o n)").rearrange("p (a k n) -> p a k n", a=2, k=KC)).then_inc(s_up, 16)
                sp.wait_ge(s_dnlo, e + 1)
                sp.dma_start(dn_raw[:], d["dn"][bass.ds(e, 1)].rearrange("o p n -> p (o n)").rearrange("p (i n) -> p i n", i=NI)).then_inc(s_dn, 16)
            with sp.Fori(0, B) as b:
                sp.wait_ge(s_fin, b + 1)
                sp.dma_start(out[bass.ds(b, 1)].rearrange("o (t p) n -> p (o t) n", p=P), X[:, bass.ds(b * TT, TT), :]).then_inc(s_out, 16)
            sp.wait_ge(s_out, 16 * B)

        @block.gpsimd
        def _(pool):
            pool.memset(half[:], -0.5).then_inc(s_const, 1)
            pool.wait_ge(s_const, 1)
            pool.sem_inc(s_add, 1)
            with pool.Fori(0, B) as b:
                pool.wait_ge(s_ms, b + 1)
                pool.tensor_tensor(rr[:], ms[:], half[:], ALU.pow).then_inc(s_r, 1)
                pool.wait_ge(s_xs, b * TT + TT)
                pool.wait_ge(s_in, b * 16 + 16)
                pool.tensor_tensor(X[:, bass.ds(b * TT, TT), :], X[:, bass.ds(b * TT, TT), :], x_in, ALU.add).then_inc(s_add, 1)
            with pool.Fori(0, B) as b:
                pool.wait_ge(s_ve, b + 1)
                pool.tensor_tensor(rstd[:], ve[:], half[:], ALU.pow).then_inc(s_rstd, 1)

        @block.scalar
        def _(act):
            act.wait_ge(s_ld, 32)
            act.activation(wr_hi[:], wr, ACT.Copy).then_inc(s_wrhi, 1)
            with act.Fori(0, B) as b:
                apart(act, s_T, b * KC + KC, s_apart)
                for t in range(TT):
                    act.activation(xs[:, t, :], one(X[:, bass.ds(b * TT + t, 1), :]), ACT.Square, accum_out=ss[:, t:t + 1]).then_inc(s_ss, 1)
                apart(act, s_r, b + 1, s_apart)
                for t in range(TT):
                    act.activation(xs[:, t, :], one(X[:, bass.ds(b * TT + t, 1), :]), ACT.Copy, scale=rr[:, t:t + 1]).then_inc(s_xs, 1)
                for k in range(KC):
                    act.wait_ge(s_T, b * KC + k + 1 + KC)
                    act.activation(h_hi[:, k, bass.ds(b * T, T)], h_bank[k], ACT.Copy, scale=w2[:, k:k + 1]).then_inc(s_hhi, 1)
            act.wait_ge(s_mid, 1)
            act.activation(prob[:], prob[:], ACT.Exp).then_inc(s_ex, 1)
            act.wait_ge(s_lc, 2 * B)
            for i in range(NE - NEXP):
                act.activation(comb[:, :, NEXP + i:NEXP + i + 1], logit[:, :, NEXP:NEXP + 1], ACT.Sigmoid).then_inc(s_sg, 1)

            def split_up(e, par):
                act.wait_ge(s_up, e * 16 + 16)
                act.activation(up_hi[:, par], up_raw[:], ACT.Copy).then_inc(s_uphi, 1)

            def split_down(e):
                act.wait_ge(s_dn, e * 16 + 16)
                act.wait_ge(s_y, e * B * TT + 1)
                act.activation(dn_hi[:], dn_raw[:], ACT.Copy).then_inc(s_dnhi, 1)

            act.wait_ge(s_add, B + 1)
            split_up(0, 0)
            split_down(0)
            with act.Fori(0, NE // 2) as pair:
                for par in range(2):
                    e = pair * 2 + par
                    for g in range(B):
                        for i, (r0, rows) in enumerate(IT):
                            n = e * B * NI + g * NI + i
                            lb = (g * NI + i) % 2
                            act.wait_ge(s_gu, n * 2 + 1)
                            act.wait_ge(s_t1, n + 1)
                            act.activation(sig[0:rows, :], gu_bank[lb][0][0:rows, :], ACT.Sigmoid).then_inc(s_sig, 1)
                            act.wait_ge(s_a, n + 3)
                            if g >= 2:
                                act.wait_ge(s_y, e * B * TT + (g - 1) * TT + 1)
                            act.activation(a_hi[0:rows, g % 2, i, :], act_f[0:rows, :], ACT.Copy).then_inc(s_ahi, 1)
                    if par == 0:
                        split_up(e + 1, 1)
                        split_down(e + 1)
                    else:
                        with act.If(pair < NE // 2 - 1):
                            split_up(e + 1, 0)
                            split_down(e + 1)

        @block.vector
        def _(dve):
            dve.sem_inc(s_uplo, 1)
            dve.sem_inc(s_dnlo, 1)
            dve.sem_inc(s_t1, 1)
            dve.sem_inc(s_a, 2)
            dve.sem_inc(s_x, TT)
            dve.sem_inc(s_hlo, KC)
            dve.wait_ge(s_wrhi, 1)
            dve.tensor_tensor(wr_lo[:], wr, wr_hi[:], ALU.subtract).then_inc(s_wr, 1)
            with dve.Fori(0, B) as b:
                dve.wait_ge(s_ss, b * TT + TT)
                dve.tensor_scalar(ms[:], ss[:], 1.0 / H, 1e-6, ALU.mult, ALU.add).then_inc(s_ms, 1)
                for k in range(KC):
                    dve.wait_ge(s_hhi, b * KC + k + 1)
                    dve.scalar_tensor_tensor(h_lo[:, k, bass.ds(b * T, T)], h_bank[k], w2[:, k:k + 1], h_hi[:, k, bass.ds(b * T, T)], ALU.mult, ALU.subtract).then_inc(s_hlo, 1)
                dve.wait_ge(s_lg, b * 2 + 1)
                dve.tensor_copy(rT[:], rT_bank).then_inc(s_lc, 1)
                dve.wait_ge(s_lg, b * 2 + 2)
                dve.tensor_copy(logit[:, bass.ds(b * TT, TT), :], r_bank.rearrange("p (t n) -> p t n", t=TT)[:, :, 0:NR]).then_inc(s_lc, 1)
            own = Count(dve, s_own)
            dve.wait_ge(s_lc, 2 * B)
            own.done(dve.tensor_reduce(small[:], logit[:, :, 0:NEXP], AX_X, ALU.max))
            own.wait()
            dve.tensor_tensor(prob[:], logit[:, :, 0:NEXP], small[:].unsqueeze(2).to_broadcast([P, NTILE, NEXP]), ALU.subtract).then_inc(s_mid, 1)
            dve.wait_ge(s_ex, 1)
            own.done(dve.tensor_reduce(small[:], prob[:], AX_X, ALU.add))
            own.wait()
            own.done(dve.reciprocal(small[:], small[:]))
            own.wait()
            own.done(dve.tensor_tensor(prob[:], prob[:], small[:].unsqueeze(2).to_broadcast([P, NTILE, NEXP]), ALU.mult))
            own.wait()
            own.done(dve.memset(rank[:], 0.0))
            own.wait()
            for j in range(NEXP):
                pj = prob[:, :, j:j + 1]
                if j:
                    own.done(dve.tensor_tensor(above[:, :, 0:j], pj.to_broadcast([P, NTILE, j]), prob[:, :, 0:j], ALU.is_gt))
                if j + 1 < NEXP:
                    own.done(dve.tensor_tensor(above[:, :, j + 1:NEXP], pj.to_broadcast([P, NTILE, NEXP - j - 1]), prob[:, :, j + 1:NEXP], ALU.is_ge))
                own.wait()
                if j:
                    own.done(dve.tensor_tensor(rank[:, :, 0:j], rank[:, :, 0:j], above[:, :, 0:j], ALU.add))
                if j + 1 < NEXP:
                    own.done(dve.tensor_tensor(rank[:, :, j + 1:NEXP], rank[:, :, j + 1:NEXP], above[:, :, j + 1:NEXP], ALU.add))
                own.wait()
            own.done(dve.tensor_scalar(above[:], rank[:], 2.0, None, ALU.is_lt))
            own.wait()
            dve.tensor_tensor(comb[:, :, 0:NEXP], prob[:], above[:], ALU.mult).then_inc(s_route, 1)
            dve.wait_ge(s_route, 1)
            dve.wait_ge(s_sg, NE - NEXP)

            def split_up(e, par):
                dve.wait_ge(s_uphi, e + 1)
                dve.tensor_tensor(up_lo[:, par], up_raw[:], up_hi[:, par], ALU.subtract).then_inc(s_uplo, 1)

            def split_down(e):
                dve.wait_ge(s_dnhi, e + 1)
                dve.tensor_tensor(dn_lo[:], dn_raw[:], dn_hi[:], ALU.subtract).then_inc(s_dnlo, 1)

            dve.wait_ge(s_add, B + 1)
            split_up(0, 0)
            split_down(0)
            with dve.Fori(0, NE // 2) as pair:
                for par in range(2):
                    e = pair * 2 + par

                    def down(g):
                        for t in range(TT):
                            q = g * TT + t
                            dve.wait_ge(s_y, e * B * TT + q + 2)
                            weight = comb[:, q:q + 1, bass.ds(e, 1)].rearrange("p o n -> p (o n)")
                            dve.scalar_tensor_tensor(X[:, q, :], y_bank[t], weight, X[:, q, :], ALU.mult, ALU.add).then_inc(s_x, 1)

                    for g in range(B):
                        for i, (r0, rows) in enumerate(IT):
                            n = e * B * NI + g * NI + i
                            gate, up = gu_bank[(g * NI + i) % 2]
                            dve.wait_ge(s_sig, n + 1)
                            dve.tensor_tensor(act_f[0:rows, :], gate[0:rows, :], sig[0:rows, :], ALU.mult).then_inc(s_t1, 1)
                            dve.wait_ge(s_t1, n + 2)
                            dve.wait_ge(s_gu, n * 2 + 2)
                            dve.tensor_tensor(act_f[0:rows, :], act_f[0:rows, :], up[0:rows, :], ALU.mult).then_inc(s_a, 1)
                            dve.wait_ge(s_ahi, n + 1)
                            dve.tensor_tensor(a_lo[0:rows, g % 2, i, :], act_f[0:rows, :], a_hi[0:rows, g % 2, i, :], ALU.subtract).then_inc(s_alo, 1)
                            if par and g == B - 1 and i == NI - 1:
                                apart(dve, s_alo, n + 1, s_apart)
                            else:
                                dve.wait_ge(s_alo, n + 1)
                            if i == 1 and g:
                                down(g - 1)
                    if par == 0:
                        split_up(e + 1, 1)
                        down(B - 1)
                        split_down(e + 1)
                    else:
                        with dve.If(pair < NE // 2 - 1):
                            split_up(e + 1, 0)
                        down(B - 1)
                        with dve.If(pair < NE // 2 - 1):
                            split_down(e + 1)
            dve.wait_ge(s_x, TT + NE * B * TT)
            with dve.Fori(0, B) as b:
                own = Count(dve, s_own2, b * 3 * TT)
                layernorm(dve, X, lambda t: b * TT + t, stats, mv, ve, rstd, own, s_ve, s_rstd, s_apart, b)
                dve.sem_inc(s_fin, 1)

        @block.tensor
        def _(pe):
            pe.sem_inc(s_T, KC)
            pe.sem_inc(s_y, 1)
            pe.wait_ge(s_wr, 1)
            with pe.Fori(0, B) as b:
                pe.wait_ge(s_xs, b * TT + TT)
                for k in range(KC):
                    pe.wait_ge(s_hlo, b * KC + k + 1)
                    for t in range(TT):
                        tr = pe.transpose(h_bank[k][:, t * P:(t + 1) * P], xs[:, t, k * P:(k + 1) * P], ident[:])
                    tr.then_inc(s_T, 1)
                pe.wait_ge(s_hlo, b * KC + 2 * KC)
                product3(pe, rT_bank, lambda c: wr_hi[:, c, :], lambda c: wr_lo[:, c, :],
                         lambda c: h_hi[:, c, bass.ds(b * T, T)], lambda c: h_lo[:, c, bass.ds(b * T, T)], KC).then_inc(s_lg, 1)
                pe.wait_ge(s_lc, b * 2 + 1)
                for t in range(TT):
                    tr = pe.transpose(r_bank[:, t * P:(t + 1) * P], rT[:, t * P:(t + 1) * P], ident[:])
                tr.then_inc(s_lg, 1)
            pe.wait_ge(s_lc, 2 * B)
            with pe.Fori(0, NE // 2) as pair:
                for par in range(2):
                    e = pair * 2 + par

                    def down(g):
                        pe.wait_ge(s_alo, e * B * NI + (g + 1) * NI)
                        pe.wait_ge(s_dnlo, e + 2)
                        for t in range(TT):
                            ts = slice(t * P, (t + 1) * P)
                            pe.wait_ge(s_x, e * B * TT + g * TT + t + 1)
                            k = 0
                            for i, (r0, rows) in enumerate(IT):
                                for a, w in ((a_hi, dn_hi), (a_hi, dn_lo), (a_lo, dn_hi)):
                                    mm = pe.matmul(y_bank[t], a[0:rows, g % 2, i, ts], w[0:rows, i, :], start=k == 0, stop=k == 3 * NI - 1)
                                    k += 1
                            mm.then_inc(s_y, 1)

                    pe.wait_ge(s_uplo, e + 2)
                    for g in range(B):
                        gs = slice(g * T, (g + 1) * T)
                        for i, (r0, rows) in enumerate(IT):
                            n = e * B * NI + g * NI + i
                            pe.wait_ge(s_a, n + 1)
                            for j in range(2):
                                product3(pe, gu_bank[(g * NI + i) % 2][j][0:rows, :],
                                         lambda c: up_hi[:, par, j, c, r0:r0 + rows], lambda c: up_lo[:, par, j, c, r0:r0 + rows],
                                         lambda c: h_hi[:, c, gs], lambda c: h_lo[:, c, gs], KC).then_inc(s_gu, 1)
                            if i == 0 and g:
                                down(g - 1)
                    down(B - 1)


def program(nc, d, out, stop_after=9):
    with ExitStack() as stack:
        m = Memory(nc, stack)
        X = m.sb("X", [P, B * TT, H])
        ident = m.sb("ident", [P, P])
        ident16 = m.sb("ident16", [P, P], BF16)
        identities(nc, ident, ident16)
        hgrn(nc, X, ident, d)
        if stop_after > 1:
            with ExitStack() as inner:
                Qn = Memory(nc, inner).sb("Qn", [P, B * TT, H])
                queries(nc, X, Qn, ident, d)
                cross_attention(nc, X, Qn, ident, ident16, d)
        if stop_after > 2:
            x0 = nc.dram_tensor("x0", (P, B * TT * H), F32).ap()
            self_attention(nc, X, x0, ident, ident16, d)
        if stop_after > 3:
            moe(nc, X, x0, ident, d, out)
            return
        s_out = m.sem("out")
        block = stack.enter_context(nc.Block())

        @block.sync
        def _(sp):
            sp.dma_start(out.rearrange("b (t p) n -> p (b t) n", p=P), X[:]).then_inc(s_out, 16)
            sp.wait_ge(s_out, 16)


def lay_out(i):
    c = np.ascontiguousarray
    a = {}
    x = np.asarray(i["x"]).reshape(B * T, H)
    a["x"] = x
    a["xT"] = c(x.T)
    for n in ("Wi", "Wf", "Wg", "Wo"):
        a[f"L0_attn_{n}"] = c(np.asarray(i[f"L0_attn_{n}"]).T)
    a["WqT"] = c(np.asarray(i["L0_xattn_Wq"]).T)
    wkv = np.concatenate([np.asarray(i["L0_xattn_Wk"]), np.asarray(i["L0_xattn_Wv"])], 0).reshape(2, HH * XD, 2, H)
    a["WkvT"] = c(wkv.transpose(0, 3, 2, 1).reshape(2, H, 2 * HH * XD))
    ctx = np.asarray(i["ctx_2048"])
    ctx = np.concatenate([ctx, np.zeros((B, CT * P - CTX, H), ctx.dtype)], 1)
    a["ctxT"] = c(ctx.reshape(B, CT, P, KC, P).transpose(0, 1, 4, 3, 2).reshape(B, CT, P, KC * P))
    a["gnorm"] = c(np.asarray(i["L0_attn_gnorm_w"]).reshape(KC, P).T)
    ffn = {k[7:]: np.asarray(v) for k, v in i.items() if k.startswith("L0_ffn_")}
    for n in ("wq", "wk", "wv", "wo"):
        a[n] = ffn[n]
    a["w1"] = c(ffn["w_ln1"].reshape(KC, P).T)
    a["w2"] = c(ffn["w_ln2"].reshape(KC, P).T)
    a["bqk"] = c(np.stack([ffn["bq"].reshape(KC, P).T, ffn["bk"].reshape(KC, P).T], 1))
    a["bv"] = c(np.broadcast_to(ffn["bv"], (P, H)))
    a["cos"], a["sin"] = rotary()
    a["wr"] = np.concatenate([ffn["w_router"], ffn["w_sh_eg"], np.zeros((H, P - NEXP - 1), np.float32)], 1)
    shared = lambda w: w.reshape(H, NE - NEXP, MI).transpose(1, 0, 2)
    gate = np.concatenate([ffn["w_gate_e"], shared(ffn["w_sh_gate"])], 0)
    up = np.concatenate([ffn["w_up_e"], shared(ffn["w_sh_up"])], 0)
    a["up"] = c(np.stack([gate, up], 1).reshape(NE, 2, KC, P, MI).transpose(0, 3, 1, 2, 4).reshape(NE, P, 2 * KC * MI))
    down = np.concatenate([ffn["w_down_e"], ffn["w_sh_down"].reshape(NE - NEXP, MI, H)], 0)
    down = np.concatenate([down, np.zeros((NE, len(IT) * P - MI, H), np.float32)], 1)
    a["dn"] = c(down.reshape(NE, len(IT), P, H).transpose(0, 2, 1, 3).reshape(NE, P, len(IT) * H))
    return a


def rotary():
    f = np.float32
    inv = f(1) / np.power(f(1000000.0), np.arange(0, SD, 2, dtype=f) / f(SD))
    angle = np.arange(T, dtype=f)[None, :] * inv[:, None]
    cos, sin = np.cos(angle), np.sin(angle)
    return (np.tile(np.concatenate([cos, cos], 0), (P // SD, 1)).astype(f),
            np.tile(np.concatenate([-sin, sin], 0), (P // SD, 1)).astype(f))


def kernel(**inputs):
    import concourse.bacc as bacc
    from concourse.bass_utils import run_bass_kernel_spmd as run

    nc = bacc.Bacc("TRN2", target_bir_lowering=False, num_devices=1)
    arrays = {f"in_{k}": v for k, v in lay_out(inputs).items()}
    d = {k[3:]: nc.dram_tensor(k, v.shape, mybir.dt.from_np(v.dtype), kind="ExternalInput").ap() for k, v in arrays.items()}
    out = nc.dram_tensor("out", (B, T, H), F32, kind="ExternalOutput").ap()
    program(nc, d, out)
    r = run(nc, [arrays], core_ids=[0])
    return r.results[0]["out"]
```

```python
from contextlib import ExitStack

import numpy as np

import concourse.bass as bass
from concourse import mybir

F32 = mybir.dt.float32
F32R = mybir.dt.float32r
BF16 = mybir.dt.bfloat16
ALU = mybir.AluOpType
ACT = mybir.ActivationFunctionType
AX_X = mybir.AxisListType.X

P = 128
B, T, H = 4, 512, 512
KC = H // P
TT = T // P
N = 512

XH, XD = 32, 16
CTX = 1601
CT = -(-CTX // P)
LAST = CTX - (CT - 1) * P
HH = XH // 2
HG = 4
NG = HH // HG
SPLIT_ROWS = 6 * XD

SH, SD = 16, 32
NEXP, MI, SI = 8, 352, 1408
NE = NEXP + SI // MI
IT = [(0, 128), (128, 128), (256, 96)]


class Count:

    def __init__(self, eng, sem, base=0):
        self.eng, self.sem, self.base, self.n = eng, sem, base, 0

    def done(self, ins):
        ins.then_inc(self.sem, 1)
        self.n += 1

    def wait(self):
        self.eng.wait_ge(self.sem, self.base + self.n)


def apart(eng, sem, value, s_apart):
    eng.wait_ge(sem, value)
    eng.sem_inc(s_apart, 1)


def one(ap):
    return ap.rearrange("p o n -> p (o n)")


class Memory:

    def __init__(self, nc, stack, tag=""):
        self.nc, self.stack, self.tag, self.sems = nc, stack, tag, []
        stack.callback(self.clear)

    def sb(self, name, shape, dt=F32):
        return self.stack.enter_context(self.nc.sbuf_tensor(self.tag + name, shape, dt))

    def banks(self):
        psum = self.stack.enter_context(self.nc.psum_tensor(self.tag + "psum", [P, 8, N], F32))
        return psum, [psum[:, i, :] for i in range(8)]

    def sem(self, *names):
        got = [self.nc.alloc_semaphore(self.tag + n) for n in names]
        self.sems += got
        return got if len(got) > 1 else got[0]

    def clear(self):
        if not self.sems:
            return
        self.nc.clear_and_free_semaphores(self.sems)
        self.nc.all_engine_barrier()


def identities(nc, ident, ident16):
    with ExitStack() as stack:
        s_id = Memory(nc, stack).sem("identity")
        block = stack.enter_context(nc.Block())

        @block.gpsimd
        def _(pool):
            for i, t in enumerate((ident, ident16)):
                pool.memset(t[:], 0.0).then_inc(s_id, 1)
                pool.wait_ge(s_id, 2 * i + 1)
                pool.affine_select(out=t[:], in_=t[:], compare_op=ALU.not_equal, fill=1.0, base=0,
                                   pattern=[[-1, P]], channel_multiplier=1).then_inc(s_id, 1)


def product3(pe, out, lhs_hi, lhs_lo, rhs_hi, rhs_lo, chunks, first=True, last=True):
    terms = [(a, b) for c in range(chunks) for a, b in ((lhs_hi, rhs_hi), (lhs_hi, rhs_lo), (lhs_lo, rhs_hi))]
    for i, (a, b) in enumerate(terms):
        c = i // 3
        mm = pe.matmul(out, a(c), b(c), start=first and i == 0, stop=last and i == len(terms) - 1)
    return mm


def batches(eng, batch):
    with eng.Fori(0, B - 1) as b:
        batch(b, False)
    batch(B - 1, True)


class LayerNorm:
    STEPS = 3 * TT

    def __init__(self, dve, X, row, tiles, own, s_ve, s_rstd, s_apart, b):
        self.dve, self.X, self.row, self.own, self.b = dve, X, row, own, b
        self.stats, self.mv, self.ve, self.rstd = tiles
        self.s_ve, self.s_rstd, self.s_apart = s_ve, s_rstd, s_apart

    def tile(self, t):
        return one(self.X[:, bass.ds(self.row(t), 1), :])

    def statistics(self, t):
        self.own.done(self.dve.bn_stats(self.stats[:, t, :], self.tile(t)))

    def variances(self):
        apart(self.dve, self.own.sem, self.own.base + self.own.n, self.s_apart)
        for t in range(TT):
            self.own.done(self.dve.bn_aggr(self.mv[:, t, :], self.stats[:, t, :]))
        self.own.wait()
        self.dve.tensor_scalar(self.ve[:], self.mv[:, :, 1], 1e-5, None, ALU.add).then_inc(self.s_ve, 1)

    def scale(self):
        self.dve.wait_ge(self.s_rstd, self.b + 1)
        for t in range(TT):
            xt = self.tile(t)
            self.own.done(self.dve.tensor_scalar(xt, xt, self.mv[:, t, 0:1], self.rstd[:, t:t + 1], ALU.subtract, ALU.mult))
        self.own.wait()

    def run(self):
        for t in range(TT):
            self.statistics(t)
        self.variances()
        self.scale()


def hgrn(nc, X, ident, d):
    with ExitStack() as stack:
        m = Memory(nc, stack, "r_")
        w_raw = [m.sb(f"w_raw{i}", [P, KC, H]) for i in range(2)]
        w_hi = [m.sb(f"w_hi{i}", [P, KC, H], F32R) for i in range(4)]
        w_lo = [m.sb(f"w_lo{i}", [P, KC, H], F32R) for i in range(4)]
        gw = m.sb("gw", [P, KC])
        x_raw = m.sb("x_raw", [P, KC, T])
        x_hi = m.sb("x_hi", [P, KC, T], F32R)
        x_lo = m.sb("x_lo", [P, KC, T], F32R)
        o_hi = m.sb("o_hi", [P, KC, T], F32R)
        o_lo = m.sb("o_lo", [P, KC, T], F32R)
        sig = m.sb("sig", [P, 2, 4, T])
        v = m.sb("v", [P, T])
        o = m.sb("o", [P, 2, T])
        sg = m.sb("sg", [P, T])
        og = m.sb("og", [P, 2, T])
        osq = m.sb("osq", [P, T])
        sumsq = m.sb("sumsq", [P, 2, T])
        ones = m.sb("ones", [P, 1])
        half = m.sb("half", [P, TT])
        ms = m.sb("ms", [P, TT])
        rr = m.sb("rr", [P, TT])
        stats = m.sb("stats", [P, TT, 6])
        mv = m.sb("mv", [P, TT, 2])
        ve = m.sb("ve", [P, TT])
        rstd = m.sb("rstd", [P, TT])
        _, bank = m.banks()
        s_apart = m.sem("apart")
        gate_bank = [bank[0:3], bank[3:6]]
        y_bank = [bank[0], bank[1], bank[2], bank[6]]
        ss_bank = bank[7]
        s_const, s_gw, s_X = m.sem("const", "gw", "X")
        s_w = m.sem(*[f"w{i}" for i in range(4)])
        s_whi, s_wlo = m.sem("whi", "wlo")
        s_x, s_xhi, s_xlo = m.sem("x", "xhi", "xlo")
        s_gate, s_sig, s_free = m.sem("gate", "sig", "free")
        s_o, s_og, s_ohi, s_olo, s_acc = m.sem("o", "og", "ohi", "olo", "acc")
        s_proj, s_y, s_ss, s_z, s_ms, s_r, s_ve, s_rstd = m.sem("proj", "y", "ss", "z", "ms", "r", "ve", "rstd")
        s_dve, s_pool = m.sem("dve", "pool")
        block = stack.enter_context(nc.Block())
        order = ["L0_attn_Wi", "L0_attn_Wf", "L0_attn_Wg", "L0_attn_Wo"]

        @block.sync
        def _(sp):
            def load_w(i):
                sp.dma_start(w_raw[i % 2][:], d[order[i]].rearrange("(k p) n -> p k n", p=P)).then_inc(s_w[i], 16)

            def load_x(b):
                src = d["xT"][:, bass.ds(b * T, T)].rearrange("(k p) n -> p k n", p=P)
                sp.dma_start(x_raw[:], src).then_inc(s_x, 16)

            load_w(0)
            load_x(0)
            load_w(1)
            sp.dma_start(gw[:], d["gnorm"]).then_inc(s_gw, 16)
            sp.dma_start(X[:], d["x"].rearrange("(t p) n -> p t n", p=P)).then_inc(s_X, 16)
            for i in (2, 3):
                sp.wait_ge(s_wlo, i - 1)
                load_w(i)
            with sp.Fori(1, B) as b:
                sp.wait_ge(s_xlo, b)
                load_x(b)

        @block.gpsimd
        def _(pool):
            pool.memset(half[:], -0.5).then_inc(s_const, 1)
            pool.wait_ge(s_const, 2)
            with pool.Fori(0, B) as b:
                own = Count(pool, s_pool, b * (KC - 1))
                for t in range(KC):
                    pool.wait_ge(s_o, b * KC + t + 1)
                    if t == 0:
                        pool.wait_ge(s_ss, b + 1)
                        pool.tensor_tensor(sumsq[:, 0, :], o[:, 0, :], o[:, 0, :], ALU.mult).then_inc(s_acc, 1)
                    else:
                        pool.wait_ge(s_acc, b * KC + t)
                        own.done(pool.tensor_tensor(osq[:], o[:, t % 2, :], o[:, t % 2, :], ALU.mult))
                        own.wait()
                        pool.tensor_tensor(sumsq[:, t % 2, :], sumsq[:, (t - 1) % 2, :], osq[:], ALU.add).then_inc(s_acc, 1)
                pool.wait_ge(s_ms, b + 1)
                pool.wait_ge(s_z, b * TT + 1)
                pool.tensor_tensor(rr[:], ms[:], half[:], ALU.pow).then_inc(s_r, 1)
                pool.wait_ge(s_ve, b + 1)
                pool.tensor_tensor(rstd[:], ve[:], half[:], ALU.pow).then_inc(s_rstd, 1)

        @block.scalar
        def _(act):
            def split_hi(i):
                act.wait_ge(s_w[i], 16)
                act.activation(w_hi[i][:], w_raw[i % 2][:], ACT.Copy).then_inc(s_whi, 1)

            def x_split(b):
                act.wait_ge(s_x, b * 16 + 16)
                act.activation(x_hi[:], x_raw[:], ACT.Copy).then_inc(s_xhi, 1)

            split_hi(0)
            x_split(0)
            for i in (1, 2, 3):
                split_hi(i)
            with act.Fori(0, B) as b:
                for t in range(KC):
                    n = b * KC + t
                    for j, (g, s) in enumerate(((0, 1.0), (1, 1.0), (1, -1.0), (2, 1.0))):
                        act.wait_ge(s_gate, n * 3 + g + 1)
                        act.wait_ge(s_free, n + 1)
                        act.activation(sig[:, t % 2, j, :], gate_bank[t % 2][g][:], ACT.Sigmoid, scale=s).then_inc(s_sig, 1)
                    act.wait_ge(s_og, n + 1)
                    act.wait_ge(s_proj, b + 1)
                    act.activation(o_hi[:, t, :], og[:, t % 2, :], ACT.Copy).then_inc(s_ohi, 1)
                with act.If(b < B - 1):
                    act.wait_ge(s_gate, (b * KC + KC) * 3)
                    x_split(b + 1)

        @block.vector
        def _(dve):
            dve.memset(ones[:], 1.0).then_inc(s_const, 1)
            dve.sem_inc(s_free, 2)
            dve.sem_inc(s_z, 1)
            dve.wait_ge(s_gw, 16)

            def split_lo(i):
                dve.wait_ge(s_whi, i + 1)
                dve.tensor_tensor(w_lo[i][:], w_raw[i % 2][:], w_hi[i][:], ALU.subtract).then_inc(s_wlo, 1)

            def x_split(b):
                dve.wait_ge(s_xhi, b + 1)
                dve.tensor_tensor(x_lo[:], x_raw[:], x_hi[:], ALU.subtract).then_inc(s_xlo, 1)

            split_lo(0)
            x_split(0)
            for i in (1, 2, 3):
                split_lo(i)
            dve.wait_ge(s_X, 16)
            per = 2 * KC + 3 * TT
            with dve.Fori(0, B) as b:
                own = Count(dve, s_dve, b * per)
                for t in range(KC):
                    n, q = b * KC + t, t % 2
                    gi, _, gg = gate_bank[q]
                    dve.wait_ge(s_sig, n * 4 + 1)
                    own.done(dve.tensor_tensor(v[:], gi[:], sig[:, q, 0, :], ALU.mult))
                    own.wait()
                    dve.wait_ge(s_sig, n * 4 + 3)
                    own.done(dve.tensor_tensor(v[:], v[:], sig[:, q, 2, :], ALU.mult))
                    own.wait()
                    if t >= 2:
                        dve.wait_ge(s_acc, n - 1)
                    dve.tensor_tensor_scan(o[:, q, :], sig[:, q, 1, :], v[:], 0.0, ALU.mult, ALU.add).then_inc(s_o, 1)
                    dve.wait_ge(s_sig, n * 4 + 4)
                    dve.tensor_tensor(sg[:], gg[:], sig[:, q, 3, :], ALU.mult).then_inc(s_free, 1)
                    dve.wait_ge(s_o, n + 1)
                    dve.wait_ge(s_free, n + 3)
                    dve.scalar_tensor_tensor(og[:, q, :], o[:, q, :], gw[:, t:t + 1], sg[:], ALU.mult, ALU.mult).then_inc(s_og, 1)
                    dve.wait_ge(s_ohi, n + 1)
                    dve.tensor_tensor(o_lo[:, t, :], og[:, q, :], o_hi[:, t, :], ALU.subtract).then_inc(s_olo, 1)
                with dve.If(b < B - 1):
                    x_split(b + 1)
                dve.wait_ge(s_ss, b + 2)
                dve.tensor_scalar(ms[:], ss_bank[:, 0:TT], 1.0 / H, 1e-5, ALU.mult, ALU.add).then_inc(s_ms, 1)
                dve.wait_ge(s_r, b + 1)
                for t in range(TT):
                    xt = one(X[:, bass.ds(b * TT + t, 1), :])
                    dve.wait_ge(s_y, b * TT + t + 1)
                    dve.scalar_tensor_tensor(xt, y_bank[t], rr[:, t:t + 1], xt, ALU.mult, ALU.add).then_inc(s_z, 1)
                apart(dve, s_z, b * TT + TT + 1, s_apart)
                LayerNorm(dve, X, lambda t: b * TT + t, (stats, mv, ve, rstd), own, s_ve, s_rstd, s_apart, b).run()
                assert own.n == per, own.n

        @block.tensor
        def _(pe):
            pe.sem_inc(s_ss, 1)
            pe.sem_inc(s_proj, 1)
            pe.wait_ge(s_const, 2)
            with pe.Fori(0, B) as b:
                pe.wait_ge(s_xlo, b + 1)
                for t in range(KC):
                    n = b * KC + t
                    pe.wait_ge(s_free, n + 1)
                    if t == 0:
                        pe.wait_ge(s_z, b * TT + 1)
                    for g in range(3):
                        if t == 0:
                            pe.wait_ge(s_wlo, g + 1)
                        product3(pe, gate_bank[t % 2][g][:],
                                 lambda c: w_hi[g][:, c, t * P:(t + 1) * P], lambda c: w_lo[g][:, c, t * P:(t + 1) * P],
                                 lambda c: x_hi[:, c, :], lambda c: x_lo[:, c, :], KC).then_inc(s_gate, 1)
                pe.wait_ge(s_olo, b * KC + KC)
                pe.wait_ge(s_wlo, 4)
                pe.wait_ge(s_free, b * KC + KC + 1)
                pe.wait_ge(s_acc, b * KC + KC)
                for t in range(TT):
                    last = pe.matmul(ss_bank[:, t:t + 1], sumsq[:, 1, t * P:(t + 1) * P], ones[:], start=t == 0, stop=True, skip_group_check=True)
                last.then_inc(s_ss, 1)
                for t in range(TT):
                    ts = slice(t * P, (t + 1) * P)
                    last = product3(pe, y_bank[t][:], lambda c: o_hi[:, c, ts], lambda c: o_lo[:, c, ts],
                                    lambda c: w_hi[3][:, c, :], lambda c: w_lo[3][:, c, :], KC)
                    last.then_inc(s_y, 1)
                pe.wait_ge(s_y, b * TT + TT)
                pe.sem_inc(s_proj, 1)


def queries(nc, X, Qn, ident, d):
    with ExitStack() as stack:
        m = Memory(nc, stack, "q_")
        w_raw = m.sb("w_raw", [P, KC, H])
        w_hi = m.sb("w_hi", [P, KC, H], F32R)
        w_lo = m.sb("w_lo", [P, KC, H], F32R)
        xs = m.sb("xs", [P, TT, H])
        x_hi = m.sb("x_hi", [P, KC, T], F32R)
        x_lo = m.sb("x_lo", [P, KC, T], F32R)
        sq = m.sb("sq", [P, 2, H])
        red = m.sb("red", [P, XH])
        ms = m.sb("ms", [P, 2, XH])
        rr = m.sb("rr", [P, 2, XH])
        half = m.sb("half", [P, XH])
        _, bank = m.banks()
        s_apart = m.sem("apart")
        s_w, s_whi, s_wlo, s_const = m.sem("w", "whi", "wlo", "const")
        s_xs, s_T, s_hi, s_lo, s_q = m.sem("xs", "T", "hi", "lo", "q")
        s_sq, s_ms, s_r, s_qn, s_dve = m.sem("sq", "ms", "r", "qn", "dve")
        block = stack.enter_context(nc.Block())

        @block.sync
        def _(sp):
            sp.dma_start(w_raw[:], d["WqT"].rearrange("(k p) n -> p k n", p=P)).then_inc(s_w, 16)

        @block.gpsimd
        def _(pool):
            pool.memset(half[:], -0.5).then_inc(s_const, 1)
            pool.wait_ge(s_const, 1)
            with pool.Fori(0, B) as b:
                for t in range(TT):
                    n = b * TT + t
                    pool.wait_ge(s_ms, n + 3)
                    pool.wait_ge(s_qn, n + 1)
                    pool.tensor_tensor(rr[:, t % 2, :], ms[:, t % 2, :], half[:], ALU.pow).then_inc(s_r, 1)

        @block.scalar
        def _(act):
            act.wait_ge(s_w, 16)
            act.activation(w_hi[:], w_raw[:], ACT.Copy).then_inc(s_whi, 1)

            def stage(b):
                act.activation(xs[:], X[:, bass.ds(b * TT, TT), :], ACT.Copy).then_inc(s_xs, 1)

            def batch(b, last):
                for k in range(KC):
                    act.wait_ge(s_T, b * KC + k + 1)
                    act.activation(x_hi[:, k, :], bank[k][:], ACT.Copy).then_inc(s_hi, 1)
                for t in range(TT):
                    act.wait_ge(s_q, b * TT + t + 1)
                    act.wait_ge(s_ms, b * TT + t + 1)
                    act.activation(sq[:, t % 2, :], bank[4 + t % 2][:], ACT.Square).then_inc(s_sq, 1)
                    if t == 1 and not last:
                        stage(b + 1)

            stage(0)
            batches(act, batch)

        @block.vector
        def _(dve):
            dve.sem_inc(s_qn, 2)
            dve.sem_inc(s_ms, 2)
            dve.wait_ge(s_whi, 1)
            dve.tensor_tensor(w_lo[:], w_raw[:], w_hi[:], ALU.subtract).then_inc(s_wlo, 1)

            def low_parts(b):
                for k in range(KC):
                    dve.wait_ge(s_hi, b * KC + k + 1)
                    dve.tensor_tensor(x_lo[:, k, :], bank[k][:], x_hi[:, k, :], ALU.subtract).then_inc(s_lo, 1)

            low_parts(0)

            def batch(b, last):
                own = Count(dve, s_dve, b * TT)

                def normalise(t):
                    dve.wait_ge(s_r, b * TT + t + 1)
                    src = bank[4 + t % 2][:].rearrange("p (h e) -> p h e", e=XD)
                    dst = one(Qn[:, bass.ds(b * TT + t, 1), :]).rearrange("p (h e) -> p h e", e=XD)
                    dve.tensor_tensor(dst, src, rr[:, t % 2, :].unsqueeze(2).to_broadcast([P, XH, XD]), ALU.mult).then_inc(s_qn, 1)

                for t in range(TT):
                    dve.wait_ge(s_sq, b * TT + t + 1)
                    own.done(dve.tensor_reduce(red[:], sq[:, t % 2, :].rearrange("p (h e) -> p h e", e=XD), AX_X, ALU.add))
                    own.wait()
                    dve.tensor_scalar(ms[:, t % 2, :], red[:], 1.0 / XD, 1e-6, ALU.mult, ALU.add).then_inc(s_ms, 1)
                    dve.wait_ge(s_ms, b * TT + t + 3)
                    if t:
                        normalise(t - 1)
                if not last:
                    low_parts(b + 1)
                normalise(TT - 1)

            batches(dve, batch)

        @block.tensor
        def _(pe):
            pe.wait_ge(s_wlo, 1)

            def turn(b):
                pe.wait_ge(s_xs, b + 1)
                for k in range(KC):
                    for t in range(TT):
                        tr = pe.transpose(bank[k][:, t * P:(t + 1) * P], xs[:, t, k * P:(k + 1) * P], ident[:])
                    tr.then_inc(s_T, 1)

            def batch(b, last):
                pe.wait_ge(s_lo, b * KC + KC)
                for t in range(TT):
                    if t == TT - 1 and not last:
                        turn(b + 1)
                    ts = slice(t * P, (t + 1) * P)
                    pe.wait_ge(s_qn, b * TT + t + 1)
                    product3(pe, bank[4 + t % 2][:], lambda c: x_hi[:, c, ts], lambda c: x_lo[:, c, ts],
                             lambda c: w_hi[:, c, :], lambda c: w_lo[:, c, :], KC).then_inc(s_q, 1)

            turn(0)
            batches(pe, batch)


def cross_attention(nc, X, Qn, ident, ident16, d):
    HW = HH * XD
    JOBS = TT + CT
    UNITS = 2 * CT
    with ExitStack() as stack:
        m = Memory(nc, stack, "c_")
        w_hi = m.sb("w_hi", [P, KC, 2 * HW], F32R)
        w_lo = m.sb("w_lo", [P, KC, 2 * HW], F32R)
        c_hi = m.sb("c_hi", [P, 2, KC, P], F32R)
        c_lo = m.sb("c_lo", [P, 2, KC, P], F32R)
        prob = m.sb("prob", [P, 2, HG, T])
        w_raw = m.sb("w_raw", [P, KC // 2, 2 * HW])
        c_raw = (m.sb("c_raw", [P, KC, P])[:], prob[:, 0, 0, :].rearrange("p (k t) -> p k t", k=KC))
        sq = m.sb("sq", [P, HW])
        red = m.sb("red", [P, HH])
        ms = m.sb("ms", [P, 3, HH])
        rr = m.sb("rr", [P, 3, HH])
        half = m.sb("half", [P, HH])
        kn = m.sb("kn", [P, 2, HW])
        rest = m.sb("rest", [P, 2, HW])
        parts = m.sb("parts", [P, 2, HH, 6, XD], BF16)
        qT = m.sb("qT", [SPLIT_ROWS, HH, T], BF16)
        kT = m.sb("kT", [SPLIT_ROWS, HH, CT * P], BF16)
        vx = m.sb("vx", [P, CT, HH, XD + 1])
        oT = m.sb("oT", [P, T])
        rec = m.sb("rec", [P, TT * HG])
        on = m.sb("on", [P, TT, HG, XD])
        half4 = m.sb("half4", [P, TT])
        stats = m.sb("stats", [P, TT, 6])
        mv = m.sb("mv", [P, TT, 2])
        ve = m.sb("ve", [P, TT])
        rstd = m.sb("rstd", [P, TT])
        psum, bank = m.banks()
        s_apart = m.sem("apart")
        kv_bank = [*bank[0:3], bank[6]]
        tr_bank = [(bank[3], bank[4]), (bank[5], bank[7])]
        score_banks = [psum[:, 2 * i:2 * i + 2, :] for i in range(3)]
        o_bank, ot_bank = bank[6], bank[7]
        s_const, s_ones, s_w, s_whi, s_wlo = m.sem("const", "ones", "w", "whi", "wlo")
        s_c = m.sem("c0", "c1")
        s_hi, s_lo, s_kv, s_sq, s_V, s_ms, s_r, s_kn = m.sem("hi", "lo", "kv", "sq", "V", "ms", "r", "kn")
        s_H, s_R, s_M, s_L, s_tr, s_ev, s_ev2 = m.sem("H", "R", "M", "L", "tr", "ev", "ev2")
        s_sc, s_ex, s_pv, s_oc, s_ot, s_xo = m.sem("sc", "ex", "pv", "oc", "ot", "xo")
        s_ve, s_rstd, s_own, s_red = m.sem("ve", "rstd", "own", "red")
        block = stack.enter_context(nc.Block())
        n_slot = [(CT + 1) // 2, CT // 2]

        def nested(eng, body, after=None):
            with eng.Fori(0, B) as b:
                with eng.Fori(0, 2) as hf:
                    body(b, hf, b * 2 + hf)
                if after:
                    after(b)

        def slots(t4, which, job):
            q = {"H": (0, 3, 1), "M": (3, 5, 1), "L": (5, 6, 1)}
            k = {"H": (1, 6, 2), "M": (2, 5, 2), "L": (0, 1, 1)}
            a, z, s = (q if job < TT else k)[which]
            return t4[:, job % 2, :, a:z:s, :]

        SPLIT, PROJECT, SQUARE, NORM, HIGH, MID, EVICT = -1, 0, 1, 3, 4, 5, 6
        STEPS = JOBS + EVICT

        def jobs(s, stage):
            return [s - stage] if 0 <= s - stage < JOBS else []

        def tiles(s, stage):
            return [(s - stage - TT, s - stage)] if TT <= s - stage < JOBS else []

        def turned_halves(j):
            for i in range(2):
                src = tr_bank[j % 2][i][:].bitcast(BF16)[0:SPLIT_ROWS, :].rearrange("p (h t) -> p h t", t=P)
                at, to = (j, qT) if j < TT else (j - TT, kT)
                yield to[:, 8 * i:8 * i + 8, at * P:(at + 1) * P], src

        def source(job, b, hf):
            if job < TT:
                ap = one(Qn[:, bass.ds(b * TT + job, 1), bass.ds(hf * HW, HW)])
            else:
                ap = kn[:, job % 2, :]
            return ap.rearrange("p (h e) -> p h e", e=XD)

        @block.sync
        def _(sp):
            def weights(half, n):
                for i in range(2):
                    apart(sp, s_wlo, n * 2 + i + 1, s_apart)
                    sp.dma_start(w_raw[:], d["WkvT"][half].rearrange("o (i k p) n -> i p (o k) n", i=2, p=P)[i]).then_inc(s_w, 16)

            weights(slice(0, 1), 0)

            def body(b, hf, it):
                for n in range(CT):
                    if n == 1:
                        sp.wait_ge(s_pv, it * NG * CT + 1)
                    if n == 0:
                        sp.wait_ge(s_lo, it * CT + 1)
                    if n >= 2:
                        sp.wait_ge(s_lo, it * CT + n)
                    sp.dma_start(c_raw[n % 2], d["ctxT"][bass.ds(b, 1), n].rearrange("o p (k t) -> p (o k) t", k=KC)
                                 ).then_inc(s_c[n % 2], 16)
                weights(bass.ds(1 - hf, 1), it + 1)
            nested(sp, body)

        @block.gpsimd
        def _(pool):
            pool.memset(half[:], -0.5).then_inc(s_const, 1)
            pool.memset(half4[:], -0.5).then_inc(s_const, 1)
            pool.sem_inc(s_wlo, 1)
            pool.wait_ge(s_const, 2)

            def weights(n):
                for i in range(2):
                    ks = slice(i * KC // 2, (i + 1) * KC // 2)
                    apart(pool, s_w, (n * 2 + i) * 16 + 16, s_apart)
                    pool.tensor_copy(w_hi[:, ks], w_raw[:]).then_inc(s_whi, 1)
                    pool.wait_ge(s_whi, n * 2 + i + 1)
                    pool.tensor_tensor(w_lo[:, ks], w_raw[:], w_hi[:, ks], ALU.subtract).then_inc(s_wlo, 1)

            weights(0)

            def body(b, hf, it):
                for n in range(CT):
                    pool.wait_ge(s_ms, it * CT + n + 1)
                    if n >= 3:
                        pool.wait_ge(s_kn, it * CT + n - 2)
                    pool.tensor_tensor(rr[:, n % 3, :], ms[:, n % 3, :], half[:], ALU.pow).then_inc(s_r, 1)
                pool.wait_ge(s_kv, it * CT + CT)
                weights(it + 1)

            def after(b):
                pool.wait_ge(s_ve, b + 1)
                pool.tensor_tensor(rstd[:], ve[:], half4[:], ALU.pow).then_inc(s_rstd, 1)
            nested(pool, body, after)

        @block.scalar
        def _(act):
            def body(b, hf, it):
                act.wait_ge(s_pv, it * NG * CT + 1)
                for s in range(STEPS + 1):
                    for n, j in tiles(s, SPLIT):
                        act.wait_ge(s_c[n % 2], (it * n_slot[n % 2] + n // 2) * 16 + 16)
                        if n >= 2:
                            act.wait_ge(s_kv, it * CT + n - 1)
                        act.activation(c_hi[:, n % 2], c_raw[n % 2], ACT.Copy).then_inc(s_hi, 1)
                    for j in jobs(s, MID):
                        act.wait_ge(s_R, it * JOBS + j + 1)
                        act.activation(slots(parts, "M", j), rest[:, j % 2, :].rearrange("p (h e) -> p h e", e=XD).unsqueeze(2).to_broadcast([P, HH, 2, XD]), ACT.Copy).then_inc(s_M, 1)
                    for j in jobs(s, HIGH):
                        if j >= TT:
                            act.wait_ge(s_kn, it * CT + j - TT + 1)
                        if j >= 2:
                            act.wait_ge(s_tr, it * JOBS + j - 1)
                        act.activation(slots(parts, "H", j), source(j, b, hf).unsqueeze(2).to_broadcast([P, HH, 3, XD]), ACT.Copy).then_inc(s_H, 1)
                    for j in jobs(s, EVICT):
                        act.wait_ge(s_tr, it * JOBS + j + 1)
                        dst, src = list(turned_halves(j))[1]
                        act.activation(dst, src, ACT.Copy).then_inc(s_ev2, 1)
                    for n, j in tiles(s, SQUARE):
                        act.wait_ge(s_kv, it * CT + n + 1)
                        if n >= 1:
                            act.wait_ge(s_red, it * CT + n)
                        act.activation(sq[:], kv_bank[n % 4][:, 0:HW], ACT.Square).then_inc(s_sq, 1)
                        act.activation(vx[:, n, :, 0:XD], kv_bank[n % 4][:, HW:2 * HW].rearrange("p (h e) -> p h e", e=XD), ACT.Copy).then_inc(s_V, 1)
                for g in range(NG):
                    for u in range(UNITS):
                        lu = g * UNITS + u
                        kt, lt = u // 2, g * CT + u // 2
                        act.wait_ge(s_sc, it * NG * UNITS + lu + 1)
                        if lt >= 2 and u % 2 == 0:
                            act.wait_ge(s_pv, it * NG * CT + lt)
                        act.activation(prob[:, lt % 2, 2 * (u % 2):2 * (u % 2) + 2, :], score_banks[lu % 3], ACT.Exp, scale=XD ** -0.5).then_inc(s_ex, 1)
            nested(act, body)

        @block.vector
        def _(dve):
            dve.memset(o_bank[:], 0.0).then_inc(s_ones, 1)
            dve.memset(vx[:, 0:CT - 1, :, XD:XD + 1], 1.0).then_inc(s_ones, 1)
            dve.memset(vx[:, CT - 1, :, XD:XD + 1], 0.0).then_inc(s_ones, 1)
            dve.wait_ge(s_ones, 3)
            dve.memset(vx[0:LAST, CT - 1, :, XD:XD + 1], 1.0).then_inc(s_ones, 1)
            dve.sem_inc(s_oc, 1)
            dve.sem_inc(s_lo, 1)
            dve.sem_inc(s_xo, 1)

            def body(b, hf, it):
                own = Count(dve, s_own, it * 2 * NG + b * 3 * TT)
                for s in range(STEPS + 1):
                    for n, j in tiles(s, SPLIT):
                        dve.wait_ge(s_hi, it * CT + n + 1)
                        if n >= 2:
                            dve.wait_ge(s_kv, it * CT + n - 1)
                        dve.tensor_tensor(c_lo[:, n % 2], c_raw[n % 2], c_hi[:, n % 2], ALU.subtract).then_inc(s_lo, 1)
                    for j in jobs(s, EVICT):
                        dve.wait_ge(s_tr, it * JOBS + j + 1)
                        dst, src = list(turned_halves(j))[0]
                        dve.tensor_copy(dst, src).then_inc(s_ev, 1)
                    for n, j in tiles(s, NORM):
                        dve.wait_ge(s_r, it * CT + n + 1)
                        dve.wait_ge(s_V, it * CT + n + 1)
                        if n >= 2:
                            dve.wait_ge(s_H, it * JOBS + j - 1)
                            dve.wait_ge(s_R, it * JOBS + j - 1)
                        dve.tensor_tensor(kn[:, j % 2, :].rearrange("p (h e) -> p h e", e=XD),
                                          kv_bank[n % 4][:, 0:HW].rearrange("p (h e) -> p h e", e=XD),
                                          rr[:, n % 3, :].unsqueeze(2).to_broadcast([P, HH, XD]), ALU.mult).then_inc(s_kn, 1)
                    for j in jobs(s, MID):
                        dve.wait_ge(s_M, it * JOBS + j + 1)
                        dve.wait_ge(s_R, it * JOBS + j + 1)
                        m0 = slots(parts, "M", j)[:, :, 0, :]
                        dve.tensor_tensor(slots(parts, "L", j)[:, :, 0, :], rest[:, j % 2, :].rearrange("p (h e) -> p h e", e=XD), m0, ALU.subtract).then_inc(s_L, 1)
                    for j in jobs(s, HIGH):
                        dve.wait_ge(s_H, it * JOBS + j + 1)
                        if j >= TT:
                            dve.wait_ge(s_kn, it * CT + j - TT + 1)
                        if j >= 2:
                            dve.wait_ge(s_L, it * JOBS + j - 1)
                        h0 = slots(parts, "H", j)[:, :, 0, :]
                        dve.tensor_tensor(rest[:, j % 2, :].rearrange("p (h e) -> p h e", e=XD), source(j, b, hf), h0, ALU.subtract).then_inc(s_R, 1)
                    for n, j in tiles(s, SQUARE):
                        dve.wait_ge(s_sq, it * CT + n + 1)
                        dve.tensor_reduce(red[:], sq[:].rearrange("p (h e) -> p h e", e=XD), AX_X, ALU.add).then_inc(s_red, 1)
                        dve.wait_ge(s_red, it * CT + n + 1)
                        if n >= 3:
                            dve.wait_ge(s_r, it * CT + n - 2)
                        dve.tensor_scalar(ms[:, n % 3, :], red[:], 1.0 / XD, 1e-6, ALU.mult, ALU.add).then_inc(s_ms, 1)
                        dve.wait_ge(s_ms, it * CT + n + 1)
                for g in range(NG):
                    gi = it * NG + g
                    dve.wait_ge(s_pv, gi * CT + CT + 1)
                    dve.tensor_copy(oT[:], o_bank[:]).then_inc(s_oc, 1)
                    dve.wait_ge(s_ot, gi + 1)
                    ot = ot_bank[:].rearrange("p (t g e) -> p t g e", t=TT, g=HG)
                    own.done(dve.reciprocal(rec[:].rearrange("p (t g) -> p t g", t=TT), ot[:, :, :, XD]))
                    own.wait()
                    own.done(dve.tensor_tensor(on[:].rearrange("p t g e -> p (t g) e"), ot_bank[:].rearrange("p (q e) -> p q e", e=32)[:, :, 0:XD],
                                               rec[:].unsqueeze(2).to_broadcast([P, TT * HG, XD]), ALU.mult))
                    own.wait()
                    xo = X[:, bass.ds(b * TT, TT), bass.ds(hf * HW + g * HG * XD, HG * XD)]
                    dve.tensor_tensor(xo, xo, on[:].rearrange("p t g e -> p t (g e)"), ALU.add).then_inc(s_xo, 1)
                    dve.wait_ge(s_xo, gi + 2)

            def after(b):
                own = Count(dve, s_own, (b * 2 + 2) * 2 * NG + b * 3 * TT)
                LayerNorm(dve, X, lambda t: b * TT + t, (stats, mv, ve, rstd), own, s_ve, s_rstd, s_apart, b).run()
            nested(dve, body, after)

        @block.tensor
        def _(pe):
            pe.sem_inc(s_pv, 1)
            pe.wait_ge(s_ones, 4)

            def body(b, hf, it):
                pe.wait_ge(s_wlo, it * 2 + 3)
                for s in range(STEPS):
                    for n, j in tiles(s, PROJECT):
                        pe.wait_ge(s_lo, it * CT + n + 2)
                        if n >= 4:
                            pe.wait_ge(s_kn, it * CT + n - 3)
                            pe.wait_ge(s_V, it * CT + n - 3)
                        product3(pe, kv_bank[n % 4][:], lambda c: c_hi[:, n % 2, c, :], lambda c: c_lo[:, n % 2, c, :],
                                 lambda c: w_hi[:, c, :], lambda c: w_lo[:, c, :], KC).then_inc(s_kv, 1)
                    for j in jobs(s, MID):
                        pe.wait_ge(s_L, it * JOBS + j + 1)
                        if j >= 2:
                            pe.wait_ge(s_ev, it * JOBS + j - 1)
                            pe.wait_ge(s_ev2, it * JOBS + j - 1)
                        for h in range(HH):
                            out = tr_bank[j % 2][h // 8][:].bitcast(BF16)[0:SPLIT_ROWS, (h % 8) * P:(h % 8 + 1) * P]
                            tr = pe.transpose(out, parts[:, j % 2, h].rearrange("p r e -> p (r e)"), ident16[:])
                        tr.then_inc(s_tr, 1)
                pe.wait_ge(s_ev, it * JOBS + JOBS)
                pe.wait_ge(s_ev2, it * JOBS + JOBS)
                pe.wait_ge(s_V, it * CT + CT)

                def scores(g, u):
                    lu = g * UNITS + u
                    if lu >= 3:
                        pe.wait_ge(s_ex, it * NG * UNITS + lu - 2)
                    for j in range(2):
                        h = g * HG + 2 * (u % 2) + j
                        mm = pe.matmul(score_banks[lu % 3][:, j, :], kT[:, h, (u // 2) * P:(u // 2 + 1) * P], qT[:, h, :], start=True, stop=True)
                    mm.then_inc(s_sc, 1)

                def turn(g):
                    gi = it * NG + g
                    pe.wait_ge(s_oc, gi + 2)
                    pe.wait_ge(s_xo, gi + 1)
                    for t in range(TT):
                        tr = pe.transpose(ot_bank[:, t * P:(t + 1) * P], oT[:, t * P:(t + 1) * P], ident[:])
                    tr.then_inc(s_ot, 1)

                for u in range(3):
                    scores(0, u)
                for lt in range(NG * CT):
                    g, kt = divmod(lt, CT)
                    for u in (2 * lt + 3, 2 * lt + 4):
                        if u < NG * UNITS:
                            scores(*divmod(u, UNITS))
                    pe.wait_ge(s_ex, it * NG * UNITS + 2 * lt + 2)
                    if kt == 0:
                        pe.wait_ge(s_oc, it * NG + g + 1)
                    for j in range(HG):
                        mm = pe.matmul(o_bank[32 * j:32 * j + XD + 1, :], vx[:, kt, g * HG + j, :], prob[:, lt % 2, j, :],
                                       start=kt == 0, stop=kt == CT - 1)
                    mm.then_inc(s_pv, 1)
                    if kt == 2 and g:
                        turn(g - 1)
                turn(NG - 1)
            nested(pe, body)


def self_attention(nc, X, x0, ident, ident16, d):
    HPC = P // SD
    PER = 2 * TT
    UNITS = KC * PER
    SCALE = SD ** -0.5
    BLOCKS = TT * (TT + 1) // 2
    with ExitStack() as stack:
        m = Memory(nc, stack, "s_")
        names = ["wq", "wk", "wv", "wo"]
        w_hi = [m.sb(f"w_hi{i}", [P, KC, H], F32R) for i in range(4)]
        w_lo = [m.sb(f"w_lo{i}", [P, KC, H], F32R) for i in range(4)]
        w1 = m.sb("w1", [P, KC])
        bqk = m.sb("bqk", [P, 2, KC])
        bv = m.sb("bv", [P, H])
        cos = m.sb("cos", [P, T])
        sin = m.sb("sin", [P, T])
        h_hi = m.sb("h_hi", [P, KC, T], F32R)
        h_lo = m.sb("h_lo", [P, KC, T], F32R)
        v = m.sb("v", [P, TT, H])
        qk = m.sb("qk", [P, T])
        turned = m.sb("turned", [P, T])
        tcos = m.sb("tcos", [P, T])
        rot = m.sb("rot", [P, 2, T])
        q_hi = m.sb("q_hi", [P, 2, T], F32R)
        q_lo = m.sb("q_lo", [P, 2, T], F32R)
        k_hi = m.sb("k_hi", [P, HPC, T], F32R)
        k_lo = m.sb("k_lo", [P, HPC, T], F32R)
        p = m.sb("p", [P, 2, 2, T])
        junk = m.sb("junk", [P, H], BF16)
        pT = m.sb("pT", [P, HPC, BLOCKS * P])
        xs = pT[:, 0:2, :].rearrange("p a n -> p (a n)")[:, 0:TT * H].rearrange("p (t n) -> p t n", t=TT)
        w_raw = pT[:, 2:4, :].rearrange("p a n -> p (a n)")[:, 0:KC * H].rearrange("p (k n) -> p k n", k=KC)
        a_hi = m.sb("a_hi", [P, KC, T], F32R)
        a_lo = m.sb("a_lo", [P, KC, T], F32R)
        w_raw = [w_raw, p[:].rearrange("p a b n -> p (a b) n"), v[:], w_raw]
        neg = m.sb("neg", [P, P], BF16)
        half = m.sb("half", [P, TT])
        ss = m.sb("ss", [P, TT])
        ms = m.sb("ms", [P, TT])
        rr = m.sb("rr", [P, TT])
        top = m.sb("top", [P, 2])
        bias = m.sb("bias", [P, 2, 2])
        rs = m.sb("rs", [P, 2, 2])
        rc = m.sb("rc", [P, 2])
        psum, bank = m.banks()
        s_apart = m.sem("apart")
        sc_banks = [psum[:, 2 * i:2 * i + 2, :] for i in range(2)]
        tr_banks, o_bank, qk_bank = psum[:, 4:6, :], bank[6], bank[7]
        h_bank, out_bank, v_bank = bank[0:4], bank[4:6], (bank[6], bank[5])
        s_const, s_zero, s_ld, s_saved = m.sem("const", "zero", "ld", "saved")
        s_w = m.sem(*[f"w{i}" for i in range(4)])
        s_whi, s_wlo = m.sem("whi", "wlo")
        s_ss, s_ms, s_r, s_xs, s_T, s_hhi, s_hlo = m.sem("ss", "ms", "r", "xs", "T", "hhi", "hlo")
        s_v, s_vs, s_qk, s_qb, s_tc, s_rot, s_turned, s_ts, s_swap = m.sem("v", "vs", "qk", "qb", "tc", "rot", "turned", "ts", "swap")
        s_qhi, s_qlo, s_khi, s_klo = m.sem("qhi", "qlo", "khi", "klo")
        s_sc, s_nb, s_ex, s_pn, s_tr, s_ev, s_top, s_rc = m.sem("sc", "nb", "ex", "pn", "tr", "ev", "top", "rc")
        s_o, s_ahi, s_alo, s_y, s_x = m.sem("o", "ahi", "alo", "y", "x")
        block = stack.enter_context(nc.Block())

        DUE = {0: [(0, 2), (0, 3)], 1: [(1, "project q")], 2: [(1, "project k")], 4: [(1, "q"), (1, 0)], 5: [(1, 1)]}
        FIRST = ("project q", "project k", "q", 0, 1, 2, 3)
        WEIGHTED, OUTPUTS = PER - 1, PER + TT - 1
        STEPS = UNITS + TT
        NEXT_SQUARES, NEXT_MEAN = UNITS - 6, UNITS - 4

        def chunk_events(n):
            c, r = divmod(n, PER)
            return [(c + dc, what) for dc, what in DUE.get(r, []) if c + dc < KC and (c or dc)]

        def unit(n):
            return n // PER, n // TT % 2, n % TT

        @block.sync
        def _(sp):
            for i in range(4):
                if i == 3:
                    sp.wait_ge(s_wlo, 1)
                sp.dma_start(w_raw[i], d[names[i]].rearrange("(k p) n -> p k n", p=P)).then_inc(s_w[i], 16)
                if i == 0:
                    for dst, src in ((w1, "w1"), (bqk, "bqk"), (bv, "bv"), (cos, "cos"), (sin, "sin")):
                        sp.dma_start(dst[:], d[src]).then_inc(s_ld, 16)
            sp.dma_start(x0.rearrange("p (t n) -> p t n", t=B * TT), X[:]).then_inc(s_saved, 16)

        @block.gpsimd
        def _(pool):
            pool.memset(half[:], -0.5).then_inc(s_const, 1)
            pool.memset(neg[:], 0.0).then_inc(s_const, 1)
            pool.wait_ge(s_const, 2)
            pool.affine_select(out=neg[:], in_=neg[:], compare_op=ALU.is_ge, fill=-1e30, base=0,
                               pattern=[[-1, P]], channel_multiplier=1).then_inc(s_const, 1)
            pool.sem_inc(s_rot, 1)
            pool.wait_ge(s_ld, 80)

            def inverse_root(b):
                pool.wait_ge(s_ms, b + 1)
                pool.tensor_tensor(rr[:], ms[:], half[:], ALU.pow).then_inc(s_r, 1)

            inverse_root(0)
            def batch(b, last):
                def event(c, what):
                    if what in ("project q", "project k"):
                        i = int(what == "project k")
                        n = b * 2 * KC + 2 * c + i
                        pool.wait_ge(s_qb, n + 1)
                        pool.wait_ge(s_rot, n + 1)
                        if c and i == 0:
                            pool.wait_ge(s_klo, (b * KC + c) * HPC)
                        pool.tensor_tensor(tcos[:], qk[:], cos[:], ALU.mult).then_inc(s_tc, 1)
                        pool.wait_ge(s_turned, n + 1)
                        if i == 0:
                            pool.tensor_tensor(turned[:], turned[:], sin[:], ALU.mult).then_inc(s_ts, 1)
                            pool.wait_ge(s_ts, b * KC + c + 1)
                        pool.wait_ge(s_tc, n + 1)
                        if c:
                            if i == 0:
                                pool.wait_ge(s_qlo, b * KC + c)
                            else:
                                pool.wait_ge(s_klo, (b * KC + c) * HPC)
                        pool.tensor_tensor(rot[:, i, :], tcos[:], turned[:], ALU.add).then_inc(s_rot, 1)
                    elif what == "q":
                        pool.wait_ge(s_qhi, b * KC + c + 1)
                        pool.tensor_tensor(q_lo[:, c % 2, :], rot[:, 0, :], q_hi[:, c % 2, :], ALU.subtract).then_inc(s_qlo, 1)
                    else:
                        r = slice(32 * what, 32 * what + 32)
                        pool.wait_ge(s_khi, (b * KC + c) * HPC + what + 1)
                        if what:
                            pool.wait_ge(s_klo, (b * KC + c) * HPC + what)
                        else:
                            pool.wait_ge(s_qlo, b * KC + c + 1)
                        pool.tensor_tensor(k_lo[r, what, :], rot[r, 1, :], k_hi[r, what, :], ALU.subtract).then_inc(s_klo, 1)

                for e in FIRST:
                    event(0, e)
                for n in range(UNITS):
                    for e in chunk_events(n):
                        event(*e)
                pool.wait_ge(s_klo, (b + 1) * KC * HPC)
                if not last:
                    inverse_root(b + 1)

            batches(pool, batch)

        @block.scalar
        def _(act):
            def high_weights(i):
                act.wait_ge(s_w[i], 16)
                act.activation(w_hi[i][:], w_raw[i], ACT.Copy).then_inc(s_whi, 1)

            def squares(b):
                for t in range(TT):
                    act.activation(junk[:], one(X[:, bass.ds(b * TT + t, 1), :]), ACT.Square, accum_out=ss[:, t:t + 1]).then_inc(s_ss, 1)
                    act.wait_ge(s_ss, b * TT + t + 1)

            def normalise(b):
                apart(act, s_r, b + 1, s_apart)
                for t in range(TT):
                    act.activation(xs[:, t, :], one(X[:, bass.ds(b * TT + t, 1), :]), ACT.Copy, scale=rr[:, t:t + 1]).then_inc(s_xs, 1)
                for k in range(KC):
                    act.wait_ge(s_T, b * KC + k + 1)
                    act.activation(h_hi[:, k, :], h_bank[k], ACT.Copy, scale=w1[:, k:k + 1]).then_inc(s_hhi, 1)

            squares(0)
            high_weights(0)
            act.wait_ge(s_ld, 80)
            normalise(0)
            for i in range(1, 4):
                high_weights(i)
            act.wait_ge(s_wlo, 4)
            act.wait_ge(s_zero, 2)
            def batch(b, last):
                def event(c, what):
                    if what in ("project q", "project k"):
                        i = what == "project k"
                        n = b * 2 * KC + 2 * c + i
                        act.wait_ge(s_qk, n + 1)
                        act.wait_ge(s_rot, n + 1)
                        act.activation(qk[:], qk_bank, ACT.Identity, bias=bqk[:, int(i), c:c + 1]).then_inc(s_qb, 1)
                    elif what == "q":
                        act.wait_ge(s_rot, b * 2 * KC + 2 * c + 2)
                        act.activation(q_hi[:, c % 2, :], rot[:, 0, :], ACT.Copy).then_inc(s_qhi, 1)
                    else:
                        r = slice(32 * what, 32 * what + 32)
                        act.wait_ge(s_rot, b * 2 * KC + 2 * c + 3)
                        if c:
                            act.wait_ge(s_sc, b * UNITS + (c - 1) * PER + (what // 2 + 1) * TT)
                        act.activation(k_hi[r, what, :], rot[r, 1, :], ACT.Copy).then_inc(s_khi, 1)

                for e in FIRST:
                    event(0, e)
                for n in range(STEPS):
                    if 0 <= (u := n - 2) < UNITS:
                        c, j, t = unit(u)
                        act.wait_ge(s_tr, b * UNITS + u + 1)
                        if j == 0 and c:
                            act.wait_ge(s_o, (b * KC + c - 1) * TT + t + 1)
                        at = t * (t + 1) // 2 * P
                        L = (t + 1) * P
                        act.activation(pT[:, 2 * j:2 * j + 2, at:at + L], tr_banks[:, :, 0:L], ACT.Copy).then_inc(s_ev, 1)
                    if n < UNITS:
                        L = (n % TT + 1) * P
                        act.wait_ge(s_nb, b * UNITS + n + 1)
                        if n >= 2:
                            act.wait_ge(s_tr, b * UNITS + n - 1)
                        for j in range(2):
                            act.activation(p[:, n % 2, j, 0:L], sc_banks[n % 2][:, j, 0:L], ACT.Exp, bias=bias[:, n % 2, j:j + 1],
                                           scale=SCALE, accum_out=rs[:, n % 2, j:j + 1]).then_inc(s_ex, 1)
                        for e in chunk_events(n):
                            event(*e)
                        if n == NEXT_SQUARES:
                            if not last:
                                squares(b + 1)
                    if n > PER and (n - OUTPUTS) % PER == 0:
                        c = (n - OUTPUTS) // PER
                        act.wait_ge(s_o, (b * KC + c + 1) * TT)
                        act.activation(a_hi[:, c, :], o_bank, ACT.Copy).then_inc(s_ahi, 1)
                if not last:
                    normalise(b + 1)

            batches(act, batch)

        @block.vector
        def _(dve):
            dve.memset(k_hi[:].bitcast(F32), 0.0).then_inc(s_zero, 1)
            dve.memset(k_lo[:].bitcast(F32), 0.0).then_inc(s_zero, 1)
            dve.sem_inc(s_x, 1)
            def low_weights(i):
                dve.wait_ge(s_whi, i + 1)
                dve.tensor_tensor(w_lo[i][:], w_raw[i], w_hi[i][:], ALU.subtract).then_inc(s_wlo, 1)

            def mean(b):
                dve.wait_ge(s_ss, b * TT + TT)
                dve.tensor_scalar(ms[:], ss[:], 1.0 / H, 1e-6, ALU.mult, ALU.add).then_inc(s_ms, 1)

            def low_parts(b):
                for k in range(KC):
                    dve.wait_ge(s_hhi, b * KC + k + 1)
                    dve.scalar_tensor_tensor(h_lo[:, k, :], h_bank[k], w1[:, k:k + 1], h_hi[:, k, :], ALU.mult, ALU.subtract).then_inc(s_hlo, 1)

            mean(0)
            low_weights(0)
            dve.wait_ge(s_ld, 80)
            low_parts(0)
            for i in range(1, 4):
                low_weights(i)
            dve.wait_ge(s_zero, 2)
            dve.wait_ge(s_saved, 16)
            def batch(b, last):
                def values(t):
                    dve.wait_ge(s_v, b * TT + t + 1)
                    dve.tensor_tensor(v[:, t, :], v_bank[t % 2], bv[:], ALU.add).then_inc(s_vs, 1)

                def shuffle(c, what):
                    n = b * 2 * KC + 2 * c + int(what == "project k")
                    dve.wait_ge(s_rot, n + 1)
                    apart(dve, s_qb, n + 1, s_apart)
                    swap = dve.stream_shuffle(turned[:], qk[:], [(r + SD // 2) % SD for r in range(SD)])
                    if what == "project q":
                        swap.then_inc(s_turned, 1)
                    else:
                        swap.then_inc(s_swap, 1)
                        dve.wait_ge(s_swap, b * KC + c + 1)
                        dve.tensor_tensor(turned[:], turned[:], sin[:], ALU.mult).then_inc(s_turned, 1)

                shuffle(0, "project q")
                values(0)
                shuffle(0, "project k")
                for t in range(1, TT):
                    values(t)
                for n in range(STEPS):
                    if n < UNITS:
                        L = (n % TT + 1) * P
                        g = b * UNITS + n
                        dve.wait_ge(s_sc, g + 1)
                        dve.reduce_max(top[:], sc_banks[n % 2][:, :, 0:L], AX_X).then_inc(s_top, 1)
                        dve.wait_ge(s_top, g + 1)
                        if n >= 2:
                            dve.wait_ge(s_ex, 2 * (g - 1))
                        dve.tensor_scalar(bias[:, n % 2, :], top[:], -SCALE, None, ALU.mult).then_inc(s_nb, 1)
                        dve.wait_ge(s_nb, g + 1)
                    if 0 <= (u := n - 1) < UNITS:
                        L = (u % TT + 1) * P
                        g = b * UNITS + u
                        dve.wait_ge(s_ex, 2 * (g + 1))
                        dve.reciprocal(rc[:], rs[:, u % 2, :]).then_inc(s_rc, 1)
                        dve.wait_ge(s_rc, g + 1)
                        pu = p[:, u % 2, :, 0:L]
                        dve.tensor_tensor(pu, pu, rc[:].unsqueeze(2).to_broadcast([P, 2, L]), ALU.mult).then_inc(s_pn, 1)
                        dve.wait_ge(s_pn, g + 1)
                    if n < UNITS:
                        for c, what in chunk_events(n - 1) if n else []:
                            if what in ("project q", "project k"):
                                shuffle(c, what)
                        if n == NEXT_MEAN:
                            if not last:
                                mean(b + 1)
                    if n > PER and (n - OUTPUTS) % PER == 0:
                        c = (n - OUTPUTS) // PER
                        dve.wait_ge(s_ahi, b * KC + c + 1)
                        dve.tensor_tensor(a_lo[:, c, :], o_bank, a_hi[:, c, :], ALU.subtract).then_inc(s_alo, 1)

                def residual(t):
                    xt = one(X[:, bass.ds(b * TT + t, 1), :])
                    dve.wait_ge(s_y, b * TT + t + 1)
                    dve.tensor_tensor(xt, xt, out_bank[t % 2], ALU.add).then_inc(s_x, 1)

                residual(0)
                residual(1)
                if not last:
                    low_parts(b + 1)
                residual(2)
                residual(3)

            batches(dve, batch)

        @block.tensor
        def _(pe):
            pe.wait_ge(s_const, 3)

            def turn(b):
                for k in range(KC):
                    for t in range(TT):
                        pe.wait_ge(s_xs, b * TT + t + 1)
                        tr = pe.transpose(h_bank[k][:, t * P:(t + 1) * P], xs[:, t, k * P:(k + 1) * P], ident[:])
                    tr.then_inc(s_T, 1)

            turn(0)
            def batch(b, last):
                pe.wait_ge(s_hlo, b * KC + KC)
                h = (lambda c: h_hi[:, c, :], lambda c: h_lo[:, c, :])
                pe.wait_ge(s_x, b * TT + 1)

                def project(c, i):
                    fs = slice(c * P, (c + 1) * P)
                    if c or i:
                        pe.wait_ge(s_qb, b * 2 * KC + 2 * c + i)
                    product3(pe, qk_bank, lambda k: w_hi[i][:, k, fs], lambda k: w_lo[i][:, k, fs], *h, KC).then_inc(s_qk, 1)

                def weighted(c, t):
                    pe.wait_ge(s_ev, b * UNITS + c * PER + TT + t + 1)
                    if c and t == 0:
                        pe.wait_ge(s_alo, b * KC + c)
                    at = t * (t + 1) // 2
                    for kt in range(t + 1):
                        for j in range(HPC):
                            hd = c * HPC + j
                            mm = pe.matmul(o_bank[32 * j:32 * j + 32, t * P:(t + 1) * P], v[:, kt, hd * SD:(hd + 1) * SD],
                                           pT[:, j, (at + kt) * P:(at + kt + 1) * P], start=kt == 0, stop=kt == t)
                    mm.then_inc(s_o, 1)

                def values(t):
                    ts = slice(t * P, (t + 1) * P)
                    if t >= 2:
                        pe.wait_ge(s_vs, b * TT + t - 1)
                    product3(pe, v_bank[t % 2], lambda c: h_hi[:, c, ts], lambda c: h_lo[:, c, ts],
                             lambda c: w_hi[2][:, c, :], lambda c: w_lo[2][:, c, :], KC).then_inc(s_v, 1)

                pe.wait_ge(s_wlo, 1)
                project(0, 0)
                pe.wait_ge(s_wlo, 4)
                values(0)
                project(0, 1)
                for t in range(1, TT):
                    values(t)
                pe.wait_ge(s_vs, b * TT + TT)
                for n in range(STEPS):
                    if n < UNITS:
                        c, pair, t = unit(n)
                        L = (t + 1) * P
                        ts = slice(t * P, L)
                        if pair == 0 and t == 0:
                            pe.wait_ge(s_qlo, b * KC + c + 1)
                        if t == 0:
                            pe.wait_ge(s_klo, (b * KC + c) * HPC + 2 * pair + 2)
                        if n >= 2:
                            pe.wait_ge(s_ex, 2 * (b * UNITS + n - 1))
                        for i in range(2):
                            j = 2 * pair + i
                            out = sc_banks[n % 2][:, i, 0:L]
                            pe.matmul(out, q_hi[:, c % 2, ts], k_hi[:, j, 0:L], start=True, stop=False)
                            pe.matmul(out, q_hi[:, c % 2, ts], k_lo[:, j, 0:L], start=False, stop=False)
                            pe.matmul(sc_banks[n % 2][:, i, ts], ident16[:], neg[:], start=False, stop=False, skip_group_check=True)
                            mm = pe.matmul(out, q_lo[:, c % 2, ts], k_hi[:, j, 0:L], start=False, stop=True)
                        mm.then_inc(s_sc, 1)
                    if 0 <= (u := n - 2) < UNITS:
                        pe.wait_ge(s_pn, b * UNITS + u + 1)
                        if u >= 1:
                            pe.wait_ge(s_ev, b * UNITS + u)
                        for i in range(2):
                            for kt in range(u % TT + 1):
                                ks = slice(kt * P, (kt + 1) * P)
                                tr = pe.transpose(tr_banks[:, i, ks], p[:, u % 2, i, ks], ident[:])
                        tr.then_inc(s_tr, 1)
                    if n < UNITS:
                        for c, what in chunk_events(n):
                            if what in ("project q", "project k"):
                                project(c, int(what == "project k"))
                    c, t = divmod(n - WEIGHTED, PER)
                    if 0 <= c < KC and t < TT:
                        weighted(c, t)
                pe.wait_ge(s_alo, b * KC + KC)
                for t in range(TT):
                    ts = slice(t * P, (t + 1) * P)
                    if t >= 2:
                        pe.wait_ge(s_x, b * TT + t)
                    product3(pe, out_bank[t % 2], lambda c: a_hi[:, c, ts], lambda c: a_lo[:, c, ts],
                             lambda c: w_hi[3][:, c, :], lambda c: w_lo[3][:, c, :], KC).then_inc(s_y, 1)
                    if t == 1:
                        if not last:
                            turn(b + 1)

            batches(pe, batch)


def moe(nc, X, x0, ident, d, out):
    NR = NEXP + 1
    with ExitStack() as stack:
        m = Memory(nc, stack, "m_")
        h_hi = m.sb("h_hi", [P, KC, B * T], F32R)
        h_lo = m.sb("h_lo", [P, KC, B * T], F32R)
        up_raw = m.sb("up_raw", [P, 2, KC, MI])
        dn_raw = m.sb("dn_raw", [P, len(IT), H])
        up_hi = m.sb("up_hi", [P, 2, 2, KC, MI], F32R)
        up_lo = m.sb("up_lo", [P, 2, 2, KC, MI], F32R)
        dn_hi = m.sb("dn_hi", [P, len(IT), H], F32R)
        dn_lo = m.sb("dn_lo", [P, len(IT), H], F32R)
        a_hi = m.sb("a_hi", [P, 2, len(IT), T], F32R)
        a_lo = m.sb("a_lo", [P, 2, len(IT), T], F32R)
        x_in = a_hi[:].bitcast(F32).rearrange("p a i n -> p (a i n)")[:, 0:TT * H].rearrange("p (t n) -> p t n", t=TT)
        work = m.sb("work", [P, 2, T])
        sig, act_f = work[:, 0], work[:, 1]
        xs = [dn_raw[:, t] for t in range(TT - 1)] + [act_f]
        rT = m.sb("rT", [P, T])
        w2 = m.sb("w2", [P, KC])
        wr = sig.rearrange("p (k n) -> p k n", k=KC)
        wr_hi = m.sb("wr_hi", [P, KC, P], F32R)
        wr_lo = m.sb("wr_lo", [P, KC, P], F32R)
        half = m.sb("half", [P, TT])
        ss = m.sb("ss", [P, TT])
        ms = m.sb("ms", [P, B * TT])
        rr = m.sb("rr", [P, TT])
        NTILE = B * TT
        logit = m.sb("logit", [P, NTILE, NR])
        prob = m.sb("prob", [P, NTILE, NEXP])
        small = m.sb("small", [P, NTILE])
        rank = m.sb("rank", [P, NTILE, NEXP])
        before = m.sb("before", [P, NEXP, NEXP])
        above, equal = (a.rearrange("p (t i j) -> p t i j", t=NTILE, i=NEXP)
                        for a in (work[:].rearrange("p a n -> p (a n)"), rT[:].bitcast(BF16)))
        comb = m.sb("comb", [P, NTILE, NE])
        stats = m.sb("stats", [P, TT, 6])
        mv = m.sb("mv", [P, TT, 2])
        ve = m.sb("ve", [P, TT])
        rstd = m.sb("rstd", [P, TT])
        _, bank = m.banks()
        s_apart = m.sem("apart")
        h_bank, rT_bank, r_bank = bank[0:4], bank[4], bank[5]
        gu_bank = [(bank[0], bank[1]), (bank[2], bank[3])]
        y_bank = bank[4:8]
        s_const, s_ld, s_wr, s_wrhi = m.sem("const", "ld", "wr", "wrhi")
        s_ss, s_ms, s_r, s_xs, s_T, s_hhi, s_hlo = m.sem("ss", "ms", "r", "xs", "T", "hhi", "hlo")
        s_lg, s_lc, s_ex, s_mid, s_sg = m.sem("lg", "lc", "ex", "mid", "sg")
        s_up, s_dn, s_uphi, s_uplo, s_dnhi, s_dnlo = m.sem("up", "dn", "uphi", "uplo", "dnhi", "dnlo")
        s_gu, s_sig, s_t1, s_a, s_ahi, s_alo, s_y, s_x = m.sem("gu", "sig", "t1", "a", "ahi", "alo", "y", "x")
        s_ve, s_rstd, s_fin, s_out, s_route, s_own2 = m.sem("ve", "rstd", "fin", "out", "route", "own2")
        s_in, s_add, s_soft = m.sem("in", "add", "soft")
        block = stack.enter_context(nc.Block())
        NI = len(IT)

        @block.sync
        def _(sp):
            def load(e):
                load_up(e)
                load_down(e)

            def load_up(e):
                sp.wait_ge(s_uplo, e + 1)
                sp.dma_start(up_raw[:], d["up"][bass.ds(e, 1)].rearrange("o p n -> p (o n)").rearrange("p (a k n) -> p a k n", a=2, k=KC)).then_inc(s_up, 16)

            def load_down(e):
                sp.wait_ge(s_dnlo, e + 1)
                sp.dma_start(dn_raw[:], d["dn"][bass.ds(e, 1)].rearrange("o p n -> p (o n)").rearrange("p (i n) -> p i n", i=NI)).then_inc(s_dn, 16)

            sp.dma_start(w2[:], d["w2"]).then_inc(s_ld, 16)
            sp.dma_start(wr, d["wr"].rearrange("(k p) n -> p k n", p=P)).then_inc(s_ld, 16)
            load_up(0)
            with sp.Fori(0, B) as b:
                sp.wait_ge(s_add, b + 1)
                sp.dma_start(x_in, x0.rearrange("p (t n) -> p t n", t=B * TT)[:, bass.ds(b * TT, TT), :]).then_inc(s_in, 16)
            sp.wait_ge(s_T, B * KC + KC)
            load_down(0)
            with sp.Fori(1, NE) as e:
                load(e)
            with sp.Fori(0, B) as b:
                sp.wait_ge(s_fin, b + 1)
                sp.dma_start(out[bass.ds(b, 1)].rearrange("o (t p) n -> p (o t) n", p=P), X[:, bass.ds(b * TT, TT), :]).then_inc(s_out, 16)
            sp.wait_ge(s_out, 16 * B)

        @block.gpsimd
        def _(pool):
            pool.memset(half[:], -0.5).then_inc(s_const, 1)
            pool.memset(before[:], 1.0).then_inc(s_const, 1)
            pool.wait_ge(s_const, 2)
            pool.affine_select(out=before[:], in_=before[:], compare_op=ALU.is_gt, fill=0.0, base=0,
                               pattern=[[1, NEXP], [-1, NEXP]], channel_multiplier=0).then_inc(s_const, 1)
            pool.sem_inc(s_add, 1)

            def inverse_root(b):
                pool.wait_ge(s_ms, b + 2)
                pool.tensor_tensor(rr[:], ms[:, bass.ds(b * TT, TT)], half[:], ALU.pow).then_inc(s_r, 1)

            def batch(b, last):
                pool.wait_ge(s_xs, b * TT + TT)
                if not last:
                    inverse_root(b + 1)
                pool.wait_ge(s_in, b * 16 + 16)
                pool.tensor_tensor(X[:, bass.ds(b * TT, TT), :], X[:, bass.ds(b * TT, TT), :], x_in, ALU.add).then_inc(s_add, 1)

            inverse_root(0)
            batches(pool, batch)
            with pool.Fori(0, B) as b:
                pool.wait_ge(s_ve, b + 1)
                pool.tensor_tensor(rstd[:], ve[:], half[:], ALU.pow).then_inc(s_rstd, 1)

        @block.scalar
        def _(act):
            act.wait_ge(s_ld, 32)
            act.activation(wr_hi[:], wr, ACT.Copy).then_inc(s_wrhi, 1)
            with act.Fori(0, B) as b:
                act.wait_ge(s_ms, b + 1)
                for t in range(TT):
                    act.activation(rT[:], one(X[:, bass.ds(b * TT + t, 1), :]), ACT.Square, accum_out=ss[:, t:t + 1]).then_inc(s_ss, 1)
                    apart(act, s_ss, b * TT + t + 1, s_apart)
            with act.Fori(0, B) as b:
                act.wait_ge(s_T, b * KC + KC)
                apart(act, s_r, b + 1, s_apart)
                for t in range(TT):
                    act.activation(xs[t], one(X[:, bass.ds(b * TT + t, 1), :]), ACT.Copy, scale=rr[:, t:t + 1]).then_inc(s_xs, 1)
                for k in range(KC):
                    act.wait_ge(s_T, b * KC + k + 1 + KC)
                    act.activation(h_hi[:, k, bass.ds(b * T, T)], h_bank[k], ACT.Copy, scale=w2[:, k:k + 1]).then_inc(s_hhi, 1)
            def split_up(e, par):
                act.wait_ge(s_up, e * 16 + 16)
                act.activation(up_hi[:, par], up_raw[:], ACT.Copy).then_inc(s_uphi, 1)

            def split_down(e):
                act.wait_ge(s_dn, e * 16 + 16)
                act.wait_ge(s_y, e * B * TT + 1)
                act.activation(dn_hi[:], dn_raw[:], ACT.Copy).then_inc(s_dnhi, 1)

            split_up(0, 0)
            split_down(0)
            act.wait_ge(s_mid, 1)
            act.activation(prob[:], prob[:], ACT.Exp).then_inc(s_ex, 1)
            act.wait_ge(s_lc, 2 * B + 1)
            for i in range(NE - NEXP):
                act.activation(comb[:, :, NEXP + i:NEXP + i + 1], logit[:, :, NEXP:NEXP + 1], ACT.Sigmoid).then_inc(s_sg, 1)
            act.wait_ge(s_add, B + 1)
            act.wait_ge(s_route, 1)
            with act.Fori(0, NE // 2) as pair:
                for par in range(2):
                    e = pair * 2 + par
                    for g in range(B):
                        for i, (r0, rows) in enumerate(IT):
                            n = e * B * NI + g * NI + i
                            lb = (g * NI + i) % 2
                            act.wait_ge(s_gu, n * 2 + 1)
                            act.wait_ge(s_t1, n + 1)
                            act.activation(sig[0:rows, :], gu_bank[lb][0][0:rows, :], ACT.Sigmoid).then_inc(s_sig, 1)
                            act.wait_ge(s_a, n + 3)
                            if g >= 2:
                                act.wait_ge(s_y, e * B * TT + (g - 1) * TT + 1)
                            act.activation(a_hi[0:rows, g % 2, i, :], act_f[0:rows, :], ACT.Copy).then_inc(s_ahi, 1)
                    if par == 0:
                        split_up(e + 1, 1)
                        split_down(e + 1)
                    else:
                        with act.If(pair < NE // 2 - 1):
                            split_up(e + 1, 0)
                            split_down(e + 1)

        @block.vector
        def _(dve):
            dve.sem_inc(s_uplo, 1)
            dve.sem_inc(s_ms, 1)
            dve.sem_inc(s_lc, 1)
            dve.sem_inc(s_dnlo, 1)
            dve.sem_inc(s_t1, 1)
            dve.sem_inc(s_a, 2)
            dve.sem_inc(s_x, TT)
            dve.sem_inc(s_hlo, KC)
            dve.wait_ge(s_wrhi, 1)
            dve.tensor_tensor(wr_lo[:], wr, wr_hi[:], ALU.subtract).then_inc(s_wr, 1)
            with dve.Fori(0, B) as b:
                dve.wait_ge(s_ss, b * TT + TT)
                dve.tensor_scalar(ms[:, bass.ds(b * TT, TT)], ss[:], 1.0 / H, 1e-6, ALU.mult, ALU.add).then_inc(s_ms, 1)
            with dve.Fori(0, B) as b:
                for k in range(KC):
                    dve.wait_ge(s_hhi, b * KC + k + 1)
                    dve.scalar_tensor_tensor(h_lo[:, k, bass.ds(b * T, T)], h_bank[k], w2[:, k:k + 1], h_hi[:, k, bass.ds(b * T, T)], ALU.mult, ALU.subtract).then_inc(s_hlo, 1)
                dve.wait_ge(s_lg, b * 2 + 1)
                dve.tensor_copy(rT[:], rT_bank).then_inc(s_lc, 1)
                dve.wait_ge(s_lg, b * 2 + 2)
                dve.tensor_copy(logit[:, bass.ds(b * TT, TT), :], r_bank.rearrange("p (t n) -> p t n", t=TT)[:, :, 0:NR]).then_inc(s_lc, 1)
            def split_up(e, par):
                dve.wait_ge(s_uphi, e + 1)
                dve.tensor_tensor(up_lo[:, par], up_raw[:], up_hi[:, par], ALU.subtract).then_inc(s_uplo, 1)

            def split_down(e):
                dve.wait_ge(s_dnhi, e + 1)
                dve.tensor_tensor(dn_lo[:], dn_raw[:], dn_hi[:], ALU.subtract).then_inc(s_dnlo, 1)

            split_up(0, 0)
            split_down(0)
            own = Count(dve, s_soft)
            dve.wait_ge(s_lc, 2 * B + 1)
            own.done(dve.tensor_reduce(small[:], logit[:, :, 0:NEXP], AX_X, ALU.max))
            own.wait()
            dve.tensor_tensor(prob[:], logit[:, :, 0:NEXP], small[:].unsqueeze(2).to_broadcast([P, NTILE, NEXP]), ALU.subtract).then_inc(s_mid, 1)
            dve.wait_ge(s_ex, 1)
            own.done(dve.tensor_reduce(small[:], prob[:], AX_X, ALU.add))
            own.wait()
            own.done(dve.reciprocal(small[:], small[:]))
            own.wait()
            own.done(dve.tensor_tensor(prob[:], prob[:], small[:].unsqueeze(2).to_broadcast([P, NTILE, NEXP]), ALU.mult))
            own.wait()
            shape = [P, NTILE, NEXP, NEXP]
            pi, pj = prob[:].unsqueeze(3).to_broadcast(shape), prob[:].unsqueeze(2).to_broadcast(shape)
            dve.wait_ge(s_const, 3)
            own.done(dve.tensor_tensor(above, pj, pi, ALU.is_gt))
            own.done(dve.tensor_tensor(equal, pj, pi, ALU.is_equal))
            own.wait()
            own.done(dve.tensor_tensor(equal, equal, before[:].unsqueeze(1).to_broadcast(shape), ALU.mult))
            own.wait()
            own.done(dve.tensor_tensor(above, above, equal, ALU.add))
            own.wait()
            own.done(dve.tensor_reduce(rank[:], above, AX_X, ALU.add))
            own.wait()
            dve.scalar_tensor_tensor(comb[:, :, 0:NEXP], rank[:], 2.0, prob[:], ALU.is_lt, ALU.mult).then_inc(s_route, 1)
            dve.wait_ge(s_add, B + 1)
            dve.wait_ge(s_route, 1)
            def experts(pair, last):
                for par in range(2):
                    e = pair * 2 + par

                    def down(g):
                        dve.wait_ge(s_sg, NE - NEXP)
                        for t in range(TT):
                            q = g * TT + t
                            dve.wait_ge(s_y, e * B * TT + q + 2)
                            weight = comb[:, q:q + 1, bass.ds(e, 1)].rearrange("p o n -> p (o n)")
                            dve.scalar_tensor_tensor(X[:, q, :], y_bank[t], weight, X[:, q, :], ALU.mult, ALU.add).then_inc(s_x, 1)
                            if last and par:
                                dve.wait_ge(s_x, TT + (NE - 1) * B * TT + q + 1)
                                norm[g].statistics(t)

                    norm = [LayerNorm(dve, X, lambda t, g=g: g * TT + t, (stats, mv, ve, rstd),
                                      Count(dve, s_own2, g * LayerNorm.STEPS), s_ve, s_rstd, s_apart, g) for g in range(B)]
                    for g in range(B):
                        for i, (r0, rows) in enumerate(IT):
                            n = e * B * NI + g * NI + i
                            gate, up = gu_bank[(g * NI + i) % 2]
                            dve.wait_ge(s_sig, n + 1)
                            dve.tensor_tensor(act_f[0:rows, :], gate[0:rows, :], sig[0:rows, :], ALU.mult).then_inc(s_t1, 1)
                            dve.wait_ge(s_t1, n + 2)
                            dve.wait_ge(s_gu, n * 2 + 2)
                            dve.tensor_tensor(act_f[0:rows, :], act_f[0:rows, :], up[0:rows, :], ALU.mult).then_inc(s_a, 1)
                            dve.wait_ge(s_ahi, n + 1)
                            dve.tensor_tensor(a_lo[0:rows, g % 2, i, :], act_f[0:rows, :], a_hi[0:rows, g % 2, i, :], ALU.subtract).then_inc(s_alo, 1)
                            dve.wait_ge(s_alo, n + 1)
                            if i == 1 and g:
                                down(g - 1)
                            if last and par and i == 2 and g:
                                norm[g - 1].variances()
                                norm[g - 1].scale()
                                dve.sem_inc(s_fin, 1)
                    if par == 0:
                        split_up(e + 1, 1)
                        down(B - 1)
                        split_down(e + 1)
                    else:
                        if not last:
                            split_up(e + 1, 0)
                        down(B - 1)
                        if not last:
                            split_down(e + 1)
            with dve.Fori(0, NE // 2 - 1) as pair:
                experts(pair, False)
            experts(NE // 2 - 1, True)
            norm = LayerNorm(dve, X, lambda t: (B - 1) * TT + t, (stats, mv, ve, rstd),
                             Count(dve, s_own2, (B - 1) * LayerNorm.STEPS + TT), s_ve, s_rstd, s_apart, B - 1)
            norm.variances()
            norm.scale()
            dve.sem_inc(s_fin, 1)

        @block.tensor
        def _(pe):
            pe.sem_inc(s_T, KC)
            pe.sem_inc(s_y, 1)
            pe.wait_ge(s_wr, 1)
            with pe.Fori(0, B) as b:
                pe.wait_ge(s_xs, b * TT + TT)
                for k in range(KC):
                    pe.wait_ge(s_hlo, b * KC + k + 1)
                    for t in range(TT):
                        tr = pe.transpose(h_bank[k][:, t * P:(t + 1) * P], xs[t][:, k * P:(k + 1) * P], ident[:])
                    tr.then_inc(s_T, 1)
                pe.wait_ge(s_hlo, b * KC + 2 * KC)
                pe.wait_ge(s_lc, b * 2 + 1)
                product3(pe, rT_bank, lambda c: wr_hi[:, c, :], lambda c: wr_lo[:, c, :],
                         lambda c: h_hi[:, c, bass.ds(b * T, T)], lambda c: h_lo[:, c, bass.ds(b * T, T)], KC).then_inc(s_lg, 1)
                pe.wait_ge(s_lc, b * 2 + 2)
                for t in range(TT):
                    tr = pe.transpose(r_bank[:, t * P:(t + 1) * P], rT[:, t * P:(t + 1) * P], ident[:])
                tr.then_inc(s_lg, 1)
            pe.wait_ge(s_lc, 2 * B + 1)
            with pe.Fori(0, NE // 2) as pair:
                for par in range(2):
                    e = pair * 2 + par

                    def down(g):
                        pe.wait_ge(s_alo, e * B * NI + (g + 1) * NI)
                        pe.wait_ge(s_dnlo, e + 2)
                        for t in range(TT):
                            ts = slice(t * P, (t + 1) * P)
                            pe.wait_ge(s_x, e * B * TT + g * TT + t + 1)
                            k = 0
                            for i, (r0, rows) in enumerate(IT):
                                for a, w in ((a_hi, dn_hi), (a_hi, dn_lo), (a_lo, dn_hi)):
                                    mm = pe.matmul(y_bank[t], a[0:rows, g % 2, i, ts], w[0:rows, i, :], start=k == 0, stop=k == 3 * NI - 1)
                                    k += 1
                            mm.then_inc(s_y, 1)

                    pe.wait_ge(s_uplo, e + 2)
                    for g in range(B):
                        gs = slice(g * T, (g + 1) * T)
                        for i, (r0, rows) in enumerate(IT):
                            n = e * B * NI + g * NI + i
                            pe.wait_ge(s_a, n + 1)
                            for j in range(2):
                                product3(pe, gu_bank[(g * NI + i) % 2][j][0:rows, :],
                                         lambda c: up_hi[:, par, j, c, r0:r0 + rows], lambda c: up_lo[:, par, j, c, r0:r0 + rows],
                                         lambda c: h_hi[:, c, gs], lambda c: h_lo[:, c, gs], KC).then_inc(s_gu, 1)
                            if i == 0 and g:
                                down(g - 1)
                    down(B - 1)


def program(nc, d, out, stop_after=9):
    with ExitStack() as stack:
        m = Memory(nc, stack)
        X = m.sb("X", [P, B * TT, H])
        ident = m.sb("ident", [P, P])
        ident16 = m.sb("ident16", [P, P], BF16)
        identities(nc, ident, ident16)
        hgrn(nc, X, ident, d)
        if stop_after > 1:
            with ExitStack() as inner:
                Qn = Memory(nc, inner).sb("Qn", [P, B * TT, H])
                queries(nc, X, Qn, ident, d)
                cross_attention(nc, X, Qn, ident, ident16, d)
        if stop_after > 2:
            x0 = nc.dram_tensor("x0", (P, B * TT * H), F32).ap()
            self_attention(nc, X, x0, ident, ident16, d)
        if stop_after > 3:
            moe(nc, X, x0, ident, d, out)
            return
        s_out = m.sem("out")
        block = stack.enter_context(nc.Block())

        @block.sync
        def _(sp):
            sp.dma_start(out.rearrange("b (t p) n -> p (b t) n", p=P), X[:]).then_inc(s_out, 16)
            sp.wait_ge(s_out, 16)


def lay_out(i):
    c = np.ascontiguousarray
    a = {}
    x = np.asarray(i["x"]).reshape(B * T, H)
    a["x"] = x
    a["xT"] = c(x.T)
    for n in ("Wi", "Wf", "Wg", "Wo"):
        a[f"L0_attn_{n}"] = c(np.asarray(i[f"L0_attn_{n}"]).T)
    a["WqT"] = c(np.asarray(i["L0_xattn_Wq"]).T)
    wkv = np.concatenate([np.asarray(i["L0_xattn_Wk"]), np.asarray(i["L0_xattn_Wv"])], 0).reshape(2, HH * XD, 2, H)
    a["WkvT"] = c(wkv.transpose(0, 3, 2, 1).reshape(2, H, 2 * HH * XD))
    ctx = np.asarray(i["ctx_2048"])
    ctx = np.concatenate([ctx, np.zeros((B, CT * P - CTX, H), ctx.dtype)], 1)
    a["ctxT"] = c(ctx.reshape(B, CT, P, KC, P).transpose(0, 1, 4, 3, 2).reshape(B, CT, P, KC * P))
    a["gnorm"] = c(np.asarray(i["L0_attn_gnorm_w"]).reshape(KC, P).T)
    ffn = {k[7:]: np.asarray(v) for k, v in i.items() if k.startswith("L0_ffn_")}
    for n in ("wq", "wk", "wv", "wo"):
        a[n] = ffn[n]
    a["w1"] = c(ffn["w_ln1"].reshape(KC, P).T)
    a["w2"] = c(ffn["w_ln2"].reshape(KC, P).T)
    a["bqk"] = c(np.stack([ffn["bq"].reshape(KC, P).T, ffn["bk"].reshape(KC, P).T], 1))
    a["bv"] = c(np.broadcast_to(ffn["bv"], (P, H)))
    a["cos"], a["sin"] = rotary()
    a["wr"] = np.concatenate([ffn["w_router"], ffn["w_sh_eg"], np.zeros((H, P - NEXP - 1), np.float32)], 1)
    shared = lambda w: w.reshape(H, NE - NEXP, MI).transpose(1, 0, 2)
    gate = np.concatenate([ffn["w_gate_e"], shared(ffn["w_sh_gate"])], 0)
    up = np.concatenate([ffn["w_up_e"], shared(ffn["w_sh_up"])], 0)
    a["up"] = c(np.stack([gate, up], 1).reshape(NE, 2, KC, P, MI).transpose(0, 3, 1, 2, 4).reshape(NE, P, 2 * KC * MI))
    down = np.concatenate([ffn["w_down_e"], ffn["w_sh_down"].reshape(NE - NEXP, MI, H)], 0)
    down = np.concatenate([down, np.zeros((NE, len(IT) * P - MI, H), np.float32)], 1)
    a["dn"] = c(down.reshape(NE, len(IT), P, H).transpose(0, 2, 1, 3).reshape(NE, P, len(IT) * H))
    return a


def rotary():
    f = np.float32
    inv = f(1) / np.power(f(1000000.0), np.arange(0, SD, 2, dtype=f) / f(SD))
    angle = np.arange(T, dtype=f)[None, :] * inv[:, None]
    cos, sin = np.cos(angle), np.sin(angle)
    return (np.tile(np.concatenate([cos, cos], 0), (P // SD, 1)).astype(f),
            np.tile(np.concatenate([-sin, sin], 0), (P // SD, 1)).astype(f))


def kernel(**inputs):
    import concourse.bacc as bacc
    from concourse.bass_utils import run_bass_kernel_spmd as run

    nc = bacc.Bacc("TRN2", target_bir_lowering=False, num_devices=1)
    arrays = {f"in_{k}": v for k, v in lay_out(inputs).items()}
    d = {k[3:]: nc.dram_tensor(k, v.shape, mybir.dt.from_np(v.dtype), kind="ExternalInput").ap() for k, v in arrays.items()}
    out = nc.dram_tensor("out", (B, T, H), F32, kind="ExternalOutput").ap()
    program(nc, d, out)
    r = run(nc, [arrays], core_ids=[0])
    return r.results[0]["out"]
```
